# Optimizing a Trainium2 kernel written in Bass

```python
import numpy as np
import jax
import jax.numpy as jnp

def _softmax(x, axis=-1):
    return jax.nn.softmax(x, axis=axis)

def _gelu(x):
    return jax.nn.gelu(x, approximate=True)

def _silu(x):
    return jax.nn.silu(x)

def _sigmoid(x):
    return jax.nn.sigmoid(x)

def _layernorm(x, axis=-1, eps=1e-05):
    m = jnp.mean(x, axis=axis, keepdims=True)
    v = jnp.var(x, axis=axis, keepdims=True)
    return (x - m) / jnp.sqrt(v + eps)

def _scatter_add(tgt, idx, src, axis=0):
    return tgt.at[idx].add(src)

def _segment_sum(src, seg, n):
    return jax.ops.segment_sum(src, seg, n)
kernel_name = 'mk_macaron_d1_jaxref_r8_0d8d45'

def setup_inputs(seed: int=0):
    np.random.seed(seed)
    _w = jnp.asarray

    def _L0_attn_setup():
        import jax, jax.numpy as jnp
        import numpy as np
        import math
        DIM_EMB = 128
        DIM_QK = 128
        DIM_V = 128
        NORM_FACT = 1.0 / math.sqrt(DIM_EMB)
        key = jax.random.key(seed)
        k0, k1, k2, k3 = jax.random.split(key, 4)
        x = jax.random.normal(k0, (4, 512, DIM_EMB), dtype=jnp.float32)
        s = 1.0 / math.sqrt(DIM_EMB)
        Wq = jax.random.uniform(k1, (DIM_QK, DIM_EMB), jnp.float32, -s, s)
        Wk = jax.random.uniform(k2, (DIM_QK, DIM_EMB), jnp.float32, -s, s)
        Wv = jax.random.uniform(k3, (DIM_V, DIM_EMB), jnp.float32, -s, s)
        return {'x': x, 'Wq': Wq, 'Wk': Wk, 'Wv': Wv}
    _L0_attn_in = _L0_attn_setup()

    def _L0_ffn_setup():
        import jax, jax.numpy as jnp
        import numpy as np
        DIM = 128
        DEPTH = 6
        HEADS = 16
        DIM_HEAD = 64
        WINDOW = 32
        INNER = HEADS * DIM_HEAD
        DIM_INNER = int(DIM * 4 * 2 / 3)
        QK_SCALE = 8.0

        def shift_tokens(t):
            a, s = jnp.split(t, 2, -1)
            s = jnp.pad(s, ((0, 0), (1, 0), (0, 0)))[:, :-1]
            return jnp.concatenate([a, s], -1)

        def l2norm(t):
            return t / jnp.maximum(jnp.linalg.norm(t, axis=-1, keepdims=True), 1e-12)

        def rotate_half(x):
            x1, x2 = jnp.split(x, 2, -1)
            return jnp.concatenate([-x2, x1], -1)

        def rotary_tables(n):
            half = jnp.arange(0, DIM_HEAD, 2, dtype=jnp.float32)
            inv_freq = 1.0 / 10000.0 ** (half / DIM_HEAD)
            t = jnp.arange(n, dtype=jnp.float32)
            freqs = t[:, None] * inv_freq[None, :]
            freqs = jnp.concatenate([freqs, freqs], -1)
            base_scale = (half + 0.4 * DIM_HEAD) / (1.4 * DIM_HEAD)
            power = (t - n // 2) / (WINDOW // 2)
            scale = base_scale[None, :] ** power[:, None]
            scale = jnp.concatenate([scale, scale], -1)
            return (freqs, scale)

        def local_attention(q, k, v):
            b, h, n, d = q.shape
            w = WINDOW
            nw = n // w
            bq = q.reshape(b, h, nw, w, d)
            bk = k.reshape(b, h, nw, w, d)
            bv = v.reshape(b, h, nw, w, d)

            def look(t):
                p = jnp.pad(t, ((0, 0), (0, 0), (1, 0), (0, 0), (0, 0)))
                return jnp.concatenate([p[:, :, :nw], p[:, :, 1:]], axis=3)
            bk2, bv2 = (look(bk), look(bv))
            seq = jnp.arange(n).reshape(nw, w)
            seq_p = jnp.pad(seq, ((1, 0), (0, 0)), constant_values=-1)
            jt = jnp.concatenate([seq_p[:nw], seq_p[1:]], axis=1)
            it = seq[:, :, None]
            jb = jt[:, None, :]
            mask = (it < jb) | (it > jb + w) | (jb == -1)
            sim = jnp.einsum('bhwie,bhwje->bhwij', bq, bk2) * QK_SCALE
            sim = jnp.where(mask, -jnp.finfo(sim.dtype).max, sim)
            attn = jax.nn.softmax(sim, -1)
            out = jnp.einsum('bhwij,bhwje->bhwie', attn, bv2)
            return out.reshape(b, h, n, d)

        def attn_layer(x, Wqkv, qs, ksc, Wo):
            b, n, _ = x.shape
            qkv = x @ Wqkv
            q, k, v = jnp.split(qkv, 3, -1)
            sh = lambda t: t.reshape(b, n, HEADS, DIM_HEAD).transpose(0, 2, 1, 3)
            q, k, v = (sh(q), sh(k), sh(v))
            q = l2norm(q) * qs
            k = l2norm(k) * ksc
            freqs, scale = rotary_tables(n)
            cos, sin = (jnp.cos(freqs), jnp.sin(freqs))
            q = q * cos * scale + rotate_half(q) * sin * scale
            inv = 1.0 / scale
            k = k * cos * inv + rotate_half(k) * sin * inv
            out = local_attention(q, k, v)
            out = out.transpose(0, 2, 1, 3).reshape(b, n, INNER)
            return out @ Wo

        def ffn_layer(x, g, bln, W1, b1, W2, b2):
            mu = x.mean(-1, keepdims=True)
            var = ((x - mu) ** 2).mean(-1, keepdims=True)
            xn = (x - mu) / jnp.sqrt(var + 1e-05) * g + bln
            hg = xn @ W1 + b1
            a, gate = jnp.split(hg, 2, -1)
            return a * jax.nn.gelu(gate, approximate=False) @ W2 + b2
        key = jax.random.key(seed)
        ks = jax.random.split(key, 8)
        B, N = (2, 256)
        init = lambda k, shape: jax.random.normal(k, shape, jnp.float32) * 0.02
        return {'x': jax.random.normal(ks[0], (B, N, DIM), jnp.float32), 'Wqkv': init(ks[1], (DEPTH, DIM, 3 * INNER)), 'q_scale': jnp.ones((DEPTH, DIM_HEAD), jnp.float32), 'k_scale': jnp.ones((DEPTH, DIM_HEAD), jnp.float32), 'Wo': init(ks[2], (DEPTH, INNER, DIM)), 'ln_g': jnp.ones((DEPTH, DIM), jnp.float32), 'ln_b': jnp.zeros((DEPTH, DIM), jnp.float32), 'W1': init(ks[3], (DEPTH, DIM, 2 * DIM_INNER)), 'b1': jnp.zeros((DEPTH, 2 * DIM_INNER), jnp.float32), 'W2': init(ks[4], (DEPTH, DIM_INNER, DIM)), 'b2': jnp.zeros((DEPTH, DIM), jnp.float32)}
    _L0_ffn_in = _L0_ffn_setup()
    _d = {'L0_attn_x': _L0_attn_in['x'], 'L0_attn_Wq': _L0_attn_in['Wq'], 'L0_attn_Wk': _L0_attn_in['Wk'], 'L0_attn_Wv': _L0_attn_in['Wv'], 'L0_ffn_Wqkv': _L0_ffn_in['Wqkv'], 'L0_ffn_q_scale': _L0_ffn_in['q_scale'], 'L0_ffn_k_scale': _L0_ffn_in['k_scale'], 'L0_ffn_Wo': _L0_ffn_in['Wo'], 'L0_ffn_ln_g': _L0_ffn_in['ln_g'], 'L0_ffn_ln_b': _L0_ffn_in['ln_b'], 'L0_ffn_W1': _L0_ffn_in['W1'], 'L0_ffn_b1': _L0_ffn_in['b1'], 'L0_ffn_W2': _L0_ffn_in['W2'], 'L0_ffn_b2': _L0_ffn_in['b2']}
    _x0 = _d['L0_attn_x']
    _d['L0_attn_x'] = jax.random.normal(jax.random.fold_in(jax.random.key(seed), 1), (2, 1024, 128), dtype=_x0.dtype)
    del _x0
    return _d

def reference(L0_attn_x, L0_attn_Wq, L0_attn_Wk, L0_attn_Wv, L0_ffn_Wqkv, L0_ffn_q_scale, L0_ffn_k_scale, L0_ffn_Wo, L0_ffn_ln_g, L0_ffn_ln_b, L0_ffn_W1, L0_ffn_b1, L0_ffn_W2, L0_ffn_b2):

    def _L0_attn_ref(x, Wq, Wk, Wv):
        import jax, jax.numpy as jnp
        import numpy as np
        import math
        DIM_EMB = 128
        DIM_QK = 128
        DIM_V = 128
        NORM_FACT = 1.0 / math.sqrt(DIM_EMB)
        q = jnp.einsum('bne,de->bnd', x, Wq)
        k = jnp.einsum('bne,de->bnd', x, Wk)
        v = jnp.einsum('bne,de->bnd', x, Wv)
        logits = jnp.einsum('bnd,bmd->bnm', q, k)
        score = jax.nn.softmax(logits, axis=-1) * NORM_FACT
        att = jnp.einsum('bnm,bmv->bnv', score, v)
        return att

    def _L0_ffn_ref(x, Wqkv, q_scale, k_scale, Wo, ln_g, ln_b, W1, b1, W2, b2):
        import jax, jax.numpy as jnp
        import numpy as np
        DIM = 128
        DEPTH = 6
        HEADS = 16
        DIM_HEAD = 64
        WINDOW = 32
        INNER = HEADS * DIM_HEAD
        DIM_INNER = int(DIM * 4 * 2 / 3)
        QK_SCALE = 8.0

        def shift_tokens(t):
            a, s = jnp.split(t, 2, -1)
            s = jnp.pad(s, ((0, 0), (1, 0), (0, 0)))[:, :-1]
            return jnp.concatenate([a, s], -1)

        def l2norm(t):
            return t / jnp.maximum(jnp.linalg.norm(t, axis=-1, keepdims=True), 1e-12)

        def rotate_half(x):
            x1, x2 = jnp.split(x, 2, -1)
            return jnp.concatenate([-x2, x1], -1)

        def rotary_tables(n):
            half = jnp.arange(0, DIM_HEAD, 2, dtype=jnp.float32)
            inv_freq = 1.0 / 10000.0 ** (half / DIM_HEAD)
            t = jnp.arange(n, dtype=jnp.float32)
            freqs = t[:, None] * inv_freq[None, :]
            freqs = jnp.concatenate([freqs, freqs], -1)
            base_scale = (half + 0.4 * DIM_HEAD) / (1.4 * DIM_HEAD)
            power = (t - n // 2) / (WINDOW // 2)
            scale = base_scale[None, :] ** power[:, None]
            scale = jnp.concatenate([scale, scale], -1)
            return (freqs, scale)

        def local_attention(q, k, v):
            b, h, n, d = q.shape
            w = WINDOW
            nw = n // w
            bq = q.reshape(b, h, nw, w, d)
            bk = k.reshape(b, h, nw, w, d)
            bv = v.reshape(b, h, nw, w, d)

            def look(t):
                p = jnp.pad(t, ((0, 0), (0, 0), (1, 0), (0, 0), (0, 0)))
                return jnp.concatenate([p[:, :, :nw], p[:, :, 1:]], axis=3)
            bk2, bv2 = (look(bk), look(bv))
            seq = jnp.arange(n).reshape(nw, w)
            seq_p = jnp.pad(seq, ((1, 0), (0, 0)), constant_values=-1)
            jt = jnp.concatenate([seq_p[:nw], seq_p[1:]], axis=1)
            it = seq[:, :, None]
            jb = jt[:, None, :]
            mask = (it < jb) | (it > jb + w) | (jb == -1)
            sim = jnp.einsum('bhwie,bhwje->bhwij', bq, bk2) * QK_SCALE
            sim = jnp.where(mask, -jnp.finfo(sim.dtype).max, sim)
            attn = jax.nn.softmax(sim, -1)
            out = jnp.einsum('bhwij,bhwje->bhwie', attn, bv2)
            return out.reshape(b, h, n, d)

        def attn_layer(x, Wqkv, qs, ksc, Wo):
            b, n, _ = x.shape
            qkv = x @ Wqkv
            q, k, v = jnp.split(qkv, 3, -1)
            sh = lambda t: t.reshape(b, n, HEADS, DIM_HEAD).transpose(0, 2, 1, 3)
            q, k, v = (sh(q), sh(k), sh(v))
            q = l2norm(q) * qs
            k = l2norm(k) * ksc
            freqs, scale = rotary_tables(n)
            cos, sin = (jnp.cos(freqs), jnp.sin(freqs))
            q = q * cos * scale + rotate_half(q) * sin * scale
            inv = 1.0 / scale
            k = k * cos * inv + rotate_half(k) * sin * inv
            out = local_attention(q, k, v)
            out = out.transpose(0, 2, 1, 3).reshape(b, n, INNER)
            return out @ Wo

        def ffn_layer(x, g, bln, W1, b1, W2, b2):
            mu = x.mean(-1, keepdims=True)
            var = ((x - mu) ** 2).mean(-1, keepdims=True)
            xn = (x - mu) / jnp.sqrt(var + 1e-05) * g + bln
            hg = xn @ W1 + b1
            a, gate = jnp.split(hg, 2, -1)
            return a * jax.nn.gelu(gate, approximate=False) @ W2 + b2
        for i in range(DEPTH):
            x = attn_layer(shift_tokens(x), Wqkv[i], q_scale[i], k_scale[i], Wo[i]) + x
            x = ffn_layer(shift_tokens(x), ln_g[i], ln_b[i], W1[i], b1[i], W2[i], b2[i]) + x
        return x
    x = L0_attn_x
    x = x + 0.5 * _L0_ffn_ref(_layernorm(x, axis=-1), L0_ffn_Wqkv, L0_ffn_q_scale, L0_ffn_k_scale, L0_ffn_Wo, L0_ffn_ln_g, L0_ffn_ln_b, L0_ffn_W1, L0_ffn_b1, L0_ffn_W2, L0_ffn_b2)
    x = x + _L0_attn_ref(_layernorm(x, axis=-1), L0_attn_Wq, L0_attn_Wk, L0_attn_Wv)
    x = x + 0.5 * _L0_ffn_ref(_layernorm(x, axis=-1), L0_ffn_Wqkv, L0_ffn_q_scale, L0_ffn_k_scale, L0_ffn_Wo, L0_ffn_ln_g, L0_ffn_ln_b, L0_ffn_W1, L0_ffn_b1, L0_ffn_W2, L0_ffn_b2)
    return x

_drawn_inputs = setup_inputs


def setup_inputs(seed=0):
    import zlib

    import numpy as np

    out = dict(_drawn_inputs(seed))
    spreads = {'L0_ffn_q_scale': (1.0, 0.6),
     'L0_ffn_k_scale': (1.0, 0.6),
     'L0_ffn_ln_g': (1.0, 0.6),
     'L0_ffn_ln_b': (0.0, 0.8),
     'L0_ffn_b1': (0.0, 0.8),
     'L0_ffn_b2': (0.0, 0.1)}
    factors = {'L0_attn_Wq': 3.255,
     'L0_attn_Wk': 3.255,
     'L0_attn_Wv': 3.228,
     'L0_ffn_W1': 3.133,
     'L0_ffn_W2': 3.075}
    for name, (base, spread) in spreads.items():
        noise = np.random.default_rng([zlib.crc32(name.encode()), seed]).standard_normal(out[name].shape)
        drawn = base * np.exp(spread * noise) if base else spread * noise
        out[name] = jnp.asarray(drawn.astype(out[name].dtype))
    for name, factor in factors.items():
        out[name] = (out[name] * factor).astype(out[name].dtype)
    return out
```

```python
import math
from contextlib import ExitStack

import numpy as np

import concourse.bass as bass
from concourse import mybir

F32 = mybir.dt.float32
BF16 = mybir.dt.bfloat16
I32 = mybir.dt.int32
ALU = mybir.AluOpType
ACT = mybir.ActivationFunctionType
AX = mybir.AxisListType

P = 128
SEQS, SEQ = 2, 1024
TPS = SEQ // P
TILES = SEQS * TPS
LAYERS = 6
HEADS, DH, WIN = 16, 64, 32
INNER = HEADS * DH
GH = 4
GROUPS = HEADS // GH
PAIRS = HEADS // 2
GW = GH * DH
SPAN = WIN + P
UNROLL = 2 * GROUPS
ITERS = TILES // 2
SLOTS = TILES * GROUPS
HID = 341
HCH = [(0, 128), (128, 128), (256, HID - 256)]
CT = 4
CHUNKS = TILES // CT
LAG_T, LAG_S, LAG_PT, LAG_AV, LAG_WO = 2, 3, 5, 6, 7
NEG = -1.0e30
MAGIC = 0x5F3759DF
NEWTON = 3
POOL_STEPS = 4 * NEWTON
NORM = 1.0 / math.sqrt(128.0)


def build(nc, x, wq, wk, wv, wqkv, qk_rows, qk_swap_rows, wo, ln_g, ln_b, w1, b1, w2, b2,
          rope_cos, rope_sin, ident, masks, out):
    with ExitStack() as ctx:
        def sb(name, shape, dt=F32):
            return ctx.enter_context(nc.sbuf_tensor(name, shape, dt))

        def ps(name):
            return ctx.enter_context(nc.psum_tensor(name, [P, 512], F32))

        def sem(name):
            return ctx.enter_context(nc.semaphore(name))

        X = sb("X", [P, TILES, P])
        XO = sb("XO", [P, TILES, P])
        XSA = sb("XSA", [P, TILES + 1, P])
        XSF = sb("XSF", [P, TILES + 1, P])
        IDF = sb("IDF", [P, P])
        IDB = sb("IDB", [P, P], BF16)
        MRAW = sb("MRAW", [P, 2, SPAN])
        MASK = sb("MASK", [P, ITERS, 2, SPAN], BF16)
        MASKO = sb("MASKO", [P, 2, SPAN], BF16)
        ROPEC = sb("ROPEC", [P, TPS, P])
        ROPES = sb("ROPES", [P, TPS, P])
        TABC = sb("TABC", [P, TPS, P])
        TABS = sb("TABS", [P, TPS, P])
        QKSC = sb("QKSC", [P, LAYERS, P])
        QKSW = sb("QKSW", [P, LAYERS, P])
        LNG = sb("LNG", [P, LAYERS])
        LNB = sb("LNB", [P, LAYERS])
        B1 = sb("B1", [P, 3, LAYERS, 2])
        B2 = sb("B2", [P, LAYERS, P])
        WQKV = sb("WQKV", [P, GROUPS, 3 * GW])
        WO = sb("WO", [P, PAIRS, P])
        W1 = sb("W1", [P, 2 * HID])
        W2 = sb("W2", [P, 3, P])
        WA = sb("WA", [P, 3, P])
        WAT = sb("WAT", [P, 3, P])
        KEEP = sb("KEEP", [P, ITERS])
        CARRY = sb("CARRY", [P, ITERS, DH])
        LVEC = sb("LVEC", [P, 2])
        BVEC = sb("BVEC", [P, 3, 2])
        B2L = sb("B2L", [P, P])
        XST = sb("XST", [P, 2, P])
        XT = sb("XT", [P, 2, P])
        SQ = sb("SQ", [P, 2, 2 * GW])
        SS = sb("SS", [P, 2, 2 * GH])
        SSC = sb("SSC", [P, 2, 2 * GH])
        SSH = sb("SSH", [P, 2, 2 * GH])
        C15 = sb("C15", [P, 2 * GH])
        HALF = sb("HALF", [P, 2, 2 * GH], I32)
        SEED = sb("SEED", [P, 2, 2 * GH])
        NT = sb("NT", [P, 2 * GH])
        RN = sb("RN", [P, UNROLL, 2 * GH])
        QKC = sb("QKC", [P, 2, 2 * GW])
        QKS = sb("QKS", [P, 2, 2 * GW])
        QKR = sb("QKR", [P, 2, 2 * GW])
        QT = sb("QT", [P, 2, 2, P])
        KT = sb("KT", [P, PAIRS, WIN + 2 * P])
        V = sb("V", [P, 2, INNER])
        VP = sb("VP", [WIN, 2, INNER])
        MX = sb("MX", [P, 2, GH])
        BIAS = sb("BIAS", [P, 2, GH])
        SUM = sb("SUM", [P, 2, GH])
        RSUM = sb("RSUM", [P, 2, GH])
        PR = sb("PR", [P, 2, GH, SPAN])
        PT = sb("PT", [P, 2, GH, P])
        PTP = sb("PTP", [WIN, 2, GH, WIN])
        OT = sb("OT", [P, 2, 2, P])
        ST = sb("ST", [P, TILES, 6])
        MV = sb("MV", [P, TILES, 2])
        LV = sb("LV", [P, TILES])
        LH = sb("LH", [P, TILES], I32)
        LT = sb("LT", [P, TILES])
        RSTD = sb("RSTD", [P, TILES])
        XN = sb("XN", [P, 2, CT, P])
        XNT = sb("XNT", [P, 2, CT * P])
        GL = sb("GL", [P, 3, CT * P])
        HT = sb("HT", [P, 2, 3, CT * P])
        YB = sb("YB", [P, 2, CT, P])
        GXT = TABC
        GQT = sb("GQT", [P, SEQ])
        GKT = sb("GKT", [P, SEQ])
        GV = sb("GV", [P, TPS, P])
        GX = TABS
        GP = V
        GPT = sb("GPT", [P, 2, SEQ])
        GMX = sb("GMX", [P, 2])
        GSUM = sb("GSUM", [P, 2])
        GRS = sb("GRS", [P, 2])

        QKP, VPS, TPS_, SA, SB_, PTPS, AVP, WOP = [ps(n) for n in ("b_qk", "b_v", "b_t", "b_sa", "b_sb", "b_pt", "b_av", "b_wo")]
        SP2 = [SA, SB_]
        XNP, YP = QKP, WOP
        GATE, LIN = [VPS, TPS_, SA], [SB_, PTPS, AVP]

        const_in = sem("const_in")
        const_ready = sem("const_ready")
        mask_ready = sem("mask_ready")
        b1_cleared = sem("b1_cleared")
        wqkv_in = sem("wqkv_in")
        ffw_in = sem("ffw_in")
        lvec_ready = sem("lvec_ready")
        tab_ready = sem("tab_ready")
        qkv_done = sem("qkv_done"); rotT_done = sem("rotT_done"); scores_done = sem("scores_done")
        probsT_done = sem("probsT_done"); av_done = sem("av_done"); wo_done = sem("wo_done")
        squared = sem("squared"); v_ready = sem("v_ready"); qkT_ready = sem("qkT_ready")
        exp_done = sem("exp_done"); outT_ready = sem("outT_ready")
        rotprod_done = sem("rotprod_done"); summed = sem("summed"); clamped = sem("clamped")
        halved = sem("halved"); seeded = sem("seeded"); max_done = sem("max_done"); bias_ready = sem("bias_ready")
        recip_done = sem("recip_done"); probs_ready = sem("probs_ready"); prevT_ready = sem("prevT_ready")
        probsT_ready = sem("probsT_ready"); vtail_ready = sem("vtail_ready")
        rot_added = sem("rot_added"); newton = sem("newton"); rot_ready = sem("rot_ready")
        xs_staged = sem("xs_staged"); xT_done = sem("xT_done"); xT_ready = sem("xT_ready")
        x_tile = sem("x_tile")
        shift_f = [sem(f"shift_f{i}") for i in range(2)]
        x_chunk = sem("x_chunk"); xn_ready = sem("xn_ready"); xnT_done = sem("xnT_done"); xnT_ready = sem("xnT_ready")
        y_done = sem("y_done"); yb_ready = sem("yb_ready")
        shift_a = [sem(f"shift_a{i}") for i in range(2)]
        w1_done = sem("w1_done"); gelu_ready = sem("gelu_ready"); hT_ready = sem("hT_ready")
        ln_link = sem("ln_link")
        carried = sem("carried"); half_f = sem("half_f"); half_a = sem("half_a")
        g_link = sem("g_link")
        outer_done = sem("outer_done")
        out_done = sem("out_done")
        waT_done = sem("waT_done"); waT_ready = sem("waT_ready"); g_xn = sem("g_xn"); g_xT = sem("g_xT"); g_xTc = sem("g_xTc")
        g_proj = sem("g_proj"); g_projc = sem("g_projc"); g_s = sem("g_s"); g_max = sem("g_max"); g_exp = sem("g_exp")
        g_pt = sem("g_pt"); g_ptc = sem("g_ptc"); g_av = sem("g_av"); g_rs = sem("g_rs"); g_out = sem("g_out")

        block = ctx.enter_context(nc.Block())
        N_CONST = 13

        def tile_of(p, j):
            return p * 2 + j // GROUPS

        def slot_loop(e, L, slots):
            slots(L, e.snap(L * ITERS), 0, True, False)
            with e.Fori(1, ITERS) as p:
                slots(L, e.snap(L * ITERS + p), p, False, False)
            slots(L, e.snap(L * ITERS + ITERS), ITERS, False, True)

        def active(j, lag, first, last):
            return not (first and j < lag) and not (last and j >= lag)

        @block.sync
        def _(sp):
            sp.dma_start(XO[:, :, :], x.rearrange("b (t p) d -> p (b t) d", p=P)).then_inc(const_in, 16)
            sp.dma_start(IDF[:, :], ident).then_inc(const_in, 16)
            sp.dma_start(MRAW[:, :, :], masks).then_inc(const_in, 16)
            sp.dma_start(ROPEC[:, :, :], rope_cos).then_inc(const_in, 16)
            sp.dma_start(ROPES[:, :, :], rope_sin).then_inc(const_in, 16)
            sp.dma_start(QKSC[:, :, :], qk_rows.partition_broadcast(P)).then_inc(const_in, 16)
            sp.dma_start(QKSW[:, :, :], qk_swap_rows.partition_broadcast(P)).then_inc(const_in, 16)
            sp.dma_start(B2[:, :, :], b2.partition_broadcast(P)).then_inc(const_in, 16)
            sp.dma_start(LNG[:, :], ln_g).then_inc(const_in, 16)
            sp.dma_start(LNB[:, :], ln_b).then_inc(const_in, 16)
            sp.wait_ge(b1_cleared, 1)
            for k, (lo, n) in enumerate(HCH):
                sp.dma_start(B1[0:n, k, :, :], b1[lo:lo + n]).then_inc(const_in, 16)

            def load_attention_weights(layer):
                src = wqkv[bass.ds(layer, 1), :, :].rearrange("a e n -> (a e) n")
                for part in range(3):
                    sp.dma_start(WQKV[:, :, part * GW:(part + 1) * GW],
                                 src[:, part * INNER:(part + 1) * INNER].rearrange("e (g c) -> e g c", g=GROUPS)).then_inc(wqkv_in, 16)
                sp.dma_start(WO[:, :, :], wo[bass.ds(layer, 1), :, :].rearrange("a (q p) n -> p (a q) n", p=P)).then_inc(wqkv_in, 16)

            def plain_wait():
                sp.wait_ge(const_in, 16 * (N_CONST + 3))

            load_attention_weights(0)
            for i, w in enumerate((wq, wk, wv)):
                sp.dma_start(WA[:, i, :], w).then_inc(const_in, 16)

            def shift_chunk(c, seen):
                sp.wait_ge(x_chunk, seen)
                plain_wait()
                t = c * CT
                sp.dma_start(XSA[1:P, t:t + CT, DH:P], X[0:P - 1, t:t + CT, DH:P]).then_inc(shift_a[c % 2], 16)
                n = CT - 1 if (t + CT) % TPS == 0 else CT
                sp.dma_start(XSA[0:1, t + 1:t + 1 + n, DH:P], X[P - 1:P, t:t + n, DH:P]).then_inc(shift_a[c % 2], 16)

            for half in range(2):
                for c in range(CHUNKS):
                    n = half * (LAYERS + 1) * CHUNKS + c
                    shift_chunk(c, n + 1)
                with sp.Fori(0, LAYERS) as l:
                    L = half * LAYERS + l
                    sp.wait_ge(x_chunk, sp.snap((half * (LAYERS + 1) + 1 + l) * CHUNKS))
                    plain_wait()
                    sp.dma_start(W1[:, :], w1[bass.ds(l, 1), :, :].rearrange("a e n -> (a e) n")).then_inc(ffw_in, 16)
                    w2l = w2[bass.ds(l, 1), :, :].rearrange("a h n -> (a h) n")
                    sp.dma_start(W2[:, 0:2, :], w2l[0:2 * P, :].rearrange("(k p) n -> p k n", p=P)).then_inc(ffw_in, 16)
                    sp.dma_start(W2[0:HID - 2 * P, 2, :], w2l[2 * P:HID, :]).then_inc(ffw_in, 16)
                    with sp.Fori(0, ITERS) as p:
                        for jt in range(2):
                            t = p * 2 + jt
                            sp.wait_ge(x_tile, sp.snap(L * TILES + p * 2 + jt + 1))
                            plain_wait()
                            sp.dma_start(XSF[1:P, bass.ds(t, 1), DH:P], X[0:P - 1, bass.ds(t, 1), DH:P]).then_inc(shift_f[jt], 16)
                            last_row = X[P - 1:P, bass.ds(t, 1), DH:P] if jt == 0 else CARRY[P - 1:P, bass.ds(p, 1), :]
                            sp.dma_start(XSF[0:1, bass.ds(t + 1, 1), DH:P], last_row).then_inc(shift_f[jt], 16)
                    sp.wait_ge(wo_done, sp.snap(L * SLOTS + SLOTS))
                    plain_wait()
                    load_attention_weights((l + 1) % LAYERS)
                    for c in range(CHUNKS):
                        n = half * (LAYERS + 1) * CHUNKS + CHUNKS + c
                        shift_chunk(c, sp.snap(l * CHUNKS + (n + 1)))
            sp.wait_ge(outer_done, 3)
            sp.dma_start(out.rearrange("b (t p) d -> p (b t) d", p=P), XO[:, :, :]).then_inc(out_done, 16)
            for c in range(2):
                sp.wait_ge(shift_a[c], 16 * CHUNKS * 2 * (LAYERS + 1))
            sp.wait_ge(wqkv_in, 64 * (2 * LAYERS + 1))
            sp.wait_ge(out_done, 16)

        @block.gpsimd
        def _(pool):
            pool.memset(B1[:, :, :, :], 0.0).then_inc(b1_cleared, 1)
            pool.memset(KEEP[:, :], 1.0).then_inc(const_ready, 1)
            pool.memset(C15[:, :], 1.5)
            pool.memset(XSA[:, :, :], 0.0).then_inc(const_ready, 1)
            pool.memset(XSF[:, :, :], 0.0).then_inc(const_ready, 1)
            pool.memset(KT[:, :, :], 0.0).then_inc(const_ready, 1)
            pool.memset(VP[:, :, :], 0.0).then_inc(const_ready, 1)
            pool.wait_ge(const_ready, 1)
            pool.memset(KEEP[:, TPS // 2 - 1:ITERS:TPS // 2], 0.0).then_inc(const_ready, 1)
            pool.wait_ge(const_in, 16 * (N_CONST + 3))
            pool.wait_ge(const_ready, 6)

            def slots(L, U, p, first, last):
                S, T = pool.snap(U * UNROLL), pool.snap(U * 2)
                N = pool.snap(S * POOL_STEPS)
                for j in range(UNROLL):
                    if not active(j, 0, first, last):
                        continue
                    b = j % 2
                    pool.wait_ge(rotprod_done, S + j + 1)
                    if not (first and j < 2):
                        pool.wait_ge(rotT_done, S + (j - 1))
                    pool.tensor_tensor(QKR[:, b, :], QKC[:, b, :], QKS[:, b, :], ALU.add).then_inc(rot_added, 1)
                    pool.wait_ge(seeded, S + j + 1)
                    if not (first and j < UNROLL):
                        pool.wait_ge(exp_done, S + (j - UNROLL + 1))
                    xx, rn = SSH[:, b, :], RN[:, j, :]
                    k = N + j * POOL_STEPS
                    for it in range(NEWTON):
                        y = SEED[:, b, :] if it == 0 else rn
                        if it:
                            pool.wait_ge(newton, k + 4 * it)
                        pool.tensor_tensor(NT[:, :], y, y, ALU.mult).then_inc(newton, 1)
                        pool.wait_ge(newton, k + 4 * it + 1)
                        pool.tensor_tensor(NT[:, :], NT[:, :], xx, ALU.mult).then_inc(newton, 1)
                        pool.wait_ge(newton, k + 4 * it + 2)
                        pool.tensor_tensor(NT[:, :], NT[:, :], C15[:, :], ALU.add).then_inc(newton, 1)
                        pool.wait_ge(newton, k + 4 * it + 3)
                        pool.tensor_tensor(rn, y, NT[:, :], ALU.mult).then_inc(newton, 1)
                    pool.wait_ge(newton, k + POOL_STEPS)
                    pool.wait_ge(rot_added, S + j + 1)
                    kk = QKR[:, b, GW:].rearrange("p (h d) -> p h d", h=GH)
                    pool.tensor_tensor(kk, kk, rn[:, GH:].unsqueeze(2).to_broadcast([P, GH, DH]), ALU.mult).then_inc(rot_ready, 1)

            for half in range(2):
                with pool.Fori(0, LAYERS) as l:
                    L = half * LAYERS + l
                    if half == 1:
                        pool.wait_ge(outer_done, 2)
                    for tab, rope, sc in ((TABC, ROPEC, QKSC), (TABS, ROPES, QKSW)):
                        pool.tensor_tensor(tab[:, :, :], rope[:, :, :], sc[:, bass.ds(l, 1), :].to_broadcast([P, TPS, P]), ALU.mult).then_inc(tab_ready, 1)
                    slot_loop(pool, L, slots)

        @block.tensor
        def _(pe):
            pe.wait_ge(const_in, 16 * (N_CONST + 3))
            pe.wait_ge(mask_ready, 2)
            pe.wait_ge(const_ready, 6)
            mm = nc.tensor.matmul

            def slots(L, U, p, first, last):
                S, T = pe.snap(U * UNROLL), pe.snap(U * 2)
                XB = pe.snap(T + L)
                for j in range(UNROLL):
                    b = j % 2
                    g, par = j % GROUPS, j // GROUPS
                    if g == 0 and not last:
                        pe.wait_ge(xs_staged, XB + par + 1)
                        if not (first and j == 0):
                            pe.wait_ge(v_ready, S + j)
                        nc.tensor.transpose(VPS[:, 256:384], XST[:, par, :], IDF[:, :]).then_inc(xT_done, 1)
                    if active(j, LAG_AV, first, last):
                        s = j - LAG_AV
                        q, sg, spar = s % 2, s % GROUPS, (s // GROUPS) % 2
                        pe.wait_ge(probsT_ready, S + (s + 1))
                        pe.wait_ge(prevT_ready, S + (s + 1))
                        pe.wait_ge(v_ready, S + (s + 1))
                        pe.wait_ge(vtail_ready, S + (s + 1))
                        if not (first and s < 1):
                            pe.wait_ge(outT_ready, S + s)
                        for i in range(GH):
                            hh, pr = i % 2, i // 2
                            col = sg * GW + i * DH
                            mm(AVP[DH * hh:DH * hh + DH, pr * P:(pr + 1) * P], V[:, spar, col:col + DH], PT[:, q, hh * 2 + pr, :],
                               start=(pr == 0), stop=False, skip_group_check=True)
                        for i in range(GH):
                            hh, pr = i % 2, i // 2
                            col = sg * GW + i * DH
                            last_av = mm(AVP[DH * hh:DH * hh + DH, pr * P:pr * P + WIN], VP[0:WIN, spar, col:col + DH], PTP[0:WIN, q, hh * 2 + pr, :],
                                         start=False, stop=True, skip_group_check=True)
                        last_av.then_inc(av_done, 1)
                    if active(j, LAG_PT, first, last):
                        s = j - LAG_PT
                        pe.wait_ge(probs_ready, S + (s + 1))
                        if not (first and s < 1):
                            pe.wait_ge(probsT_ready, S + s)
                        for i in range(GH):
                            last_pt = nc.tensor.transpose(PTPS[:, i * P:(i + 1) * P], PR[:, s % 2, i, WIN:SPAN], IDF[:, :])
                        last_pt.then_inc(probsT_done, 1)
                    if active(j, LAG_T, first, last):
                        s = j - LAG_T
                        pe.wait_ge(rot_ready, S + (s + 1))
                        if not (first and s < 1):
                            pe.wait_ge(qkT_ready, S + s)
                        for i in range(4):
                            last_t = nc.tensor.transpose(TPS_[:, i * P:(i + 1) * P], QKR[:, s % 2, i * P:(i + 1) * P], IDF[:, :])
                        last_t.then_inc(rotT_done, 1)
                    if active(j, LAG_S, first, last):
                        s = j - LAG_S
                        sg, spar = s % GROUPS, (s // GROUPS) % 2
                        pe.wait_ge(qkT_ready, S + (s + 1))
                        if not (first and s < 1):
                            pe.wait_ge(exp_done, S + s)
                        if spar:
                            m = MASKO[:, :, :]
                        else:
                            m = MASK[:, bass.ds(p + (s // UNROLL), 1), :, :].rearrange("p a h c -> p (a h) c")
                        for hh in range(2):
                            mm(SP2[hh][:, 0:2 * SPAN], IDB[:, :], m.rearrange("p h c -> p (h c)"), start=True, stop=False, skip_group_check=True)
                        for i in range(GH):
                            hh, pr = i % 2, i // 2
                            last_s = mm(SP2[hh][:, pr * SPAN:(pr + 1) * SPAN], QT[DH * hh:DH * hh + DH, s % 2, pr, :],
                                        KT[DH * hh:DH * hh + DH, sg * 2 + pr, spar * P:spar * P + SPAN],
                                        start=False, stop=True, skip_group_check=True)
                        last_s.then_inc(scores_done, 1)
                    if active(j, LAG_WO, first, last):
                        s = j - LAG_WO
                        sg = s % GROUPS
                        pe.wait_ge(outT_ready, S + (s + 1))
                        if sg == 0 and not (first and s < GROUPS):
                            pe.wait_ge(x_tile, T + (s // GROUPS))
                        for pr in range(2):
                            last_wo = mm(WOP[:, 0:P], OT[:, s % 2, pr, :], WO[:, sg * 2 + pr, :],
                                         start=(sg == 0 and pr == 0), stop=(sg == GROUPS - 1 and pr == 1), skip_group_check=True)
                        last_wo.then_inc(wo_done, 1)
                    if not last:
                        if g == 0:
                            pe.wait_ge(xT_ready, T + par + 1)
                        if not (first and j < 1):
                            pe.wait_ge(rotprod_done, S + j)
                            pe.wait_ge(squared, S + j)
                            pe.wait_ge(v_ready, S + j)
                        mm(QKP[:, :], XT[:, par, :], WQKV[:, g, 0:2 * GW], start=True, stop=True)
                        mm(VPS[:, 0:GW], XT[:, par, :], WQKV[:, g, 2 * GW:], start=True, stop=True).then_inc(qkv_done, 1)

            def ffn(L):
                C, C3 = pe.snap(L * CHUNKS), pe.snap(L * (3 * CHUNKS))
                pe.wait_ge(ffw_in, pe.snap(L * 48 + 48))

                def to_features(c):
                    pe.wait_ge(xn_ready, C + (c + 1))
                    if c:
                        pe.wait_ge(xnT_ready, C + c)
                    for i in range(CT):
                        t = nc.tensor.transpose(XNP[:, i * P:(i + 1) * P], XN[:, c % 2, i, :], IDF[:, :])
                    t.then_inc(xnT_done, 1)

                def up(c):
                    pe.wait_ge(xnT_ready, C + (c + 1))
                    for k, (lo, n) in enumerate(HCH):
                        if c:
                            pe.wait_ge(hT_ready, C3 + (3 * (c - 1) + k + 1))
                        mm(GATE[k][0:n, :], W1[:, HID + lo:HID + lo + n], XNT[:, c % 2, :], start=True, stop=True)
                        mm(LIN[k][0:n, :], W1[:, lo:lo + n], XNT[:, c % 2, :], start=True, stop=True).then_inc(w1_done, 1)

                def down(c):
                    pe.wait_ge(hT_ready, C3 + (3 * c + 3))
                    if c:
                        pe.wait_ge(yb_ready, C + c)
                    for i in range(CT):
                        for k, (lo, n) in enumerate(HCH):
                            y = mm(YP[:, i * P:(i + 1) * P], HT[0:n, c % 2, k, i * P:(i + 1) * P], W2[0:n, k, :],
                                   start=(k == 0), stop=(k == 2))
                    y.then_inc(y_done, 1)

                to_features(0)
                for c in range(CHUNKS):
                    up(c)
                    if c + 1 < CHUNKS:
                        to_features(c + 1)
                    if c:
                        down(c - 1)
                down(CHUNKS - 1)

            def global_attention():
                for i in range(3):
                    t = nc.tensor.transpose(SA[:, i * P:(i + 1) * P], WA[:, i, :], IDF[:, :])
                t.then_inc(waT_done, 1)
                pe.wait_ge(waT_ready, 1)
                with pe.Fori(0, SEQS) as q:
                    G = pe.snap(q * TPS)
                    pe.wait_ge(g_xn, q + 1)
                    for i in range(TPS):
                        t = nc.tensor.transpose(SP2[i // 4][:, (i % 4) * P:(i % 4 + 1) * P], GX[:, i, :], IDF[:, :])
                    t.then_inc(g_xT, 1)
                    pe.wait_ge(g_xTc, q * 2 + 2)
                    for i in range(2):
                        for n in range(2):
                            t = mm([QKP, VPS, TPS_, PTPS][2 * i + n][:, :], WAT[:, i, :], GXT[:, 4 * n:4 * n + 4, :].rearrange("p a b -> p (a b)"), start=True, stop=True)
                    for i in range(TPS):
                        t = mm([AVP, WOP][i // 4][:, (i % 4) * P:(i % 4 + 1) * P], GXT[:, i, :], WAT[:, 2, :], start=True, stop=True)
                    t.then_inc(g_proj, 1)
                    pe.wait_ge(g_projc, q * 6 + 6)

                    def scores(i):
                        for n in range(2):
                            t = mm([[SA, SB_], [QKP, VPS]][i % 2][n][:, :], GQT[:, i * P:(i + 1) * P], GKT[:, n * 512:(n + 1) * 512], start=True, stop=True)
                        t.then_inc(g_s, 1)

                    scores(0)
                    for i in range(TPS):
                        if i + 1 < TPS:
                            if i >= 1:
                                pe.wait_ge(g_exp, G + i)
                            scores(i + 1)
                        pe.wait_ge(g_exp, G + (i + 1))
                        if i:
                            pe.wait_ge(g_ptc, pe.snap(q * (2 * TPS) + 2 * i))
                        for k in range(TPS):
                            t = nc.tensor.transpose([TPS_, PTPS][k // 4][:, (k % 4) * P:(k % 4 + 1) * P], GP[:, i % 2, k * P:(k + 1) * P], IDF[:, :])
                        t.then_inc(g_pt, 1)
                        pe.wait_ge(g_ptc, pe.snap(q * (2 * TPS) + 2 * i + 2))
                        if i:
                            pe.wait_ge(g_out, G + i)
                        for k in range(TPS):
                            t = mm(AVP[:, 0:P], GPT[:, i % 2, k * P:(k + 1) * P], GV[:, k, :], start=(k == 0), stop=(k == TPS - 1))
                        t.then_inc(g_av, 1)
                    pe.wait_ge(g_out, G + TPS)

            for half in range(2):
                if half == 1:
                    pe.wait_ge(outer_done, 1)
                    global_attention()
                with pe.Fori(0, LAYERS) as l:
                    L = half * LAYERS + l
                    pe.wait_ge(wqkv_in, pe.snap(L * 64 + 64))
                    slot_loop(pe, L, slots)
                    ffn(L)

        @block.scalar
        def _(act):
            A = nc.scalar.activation
            act.wait_ge(const_ready, 6)

            def slots(L, U, p, first, last):
                S, T = act.snap(U * UNROLL), act.snap(U * 2)
                for j in range(UNROLL):
                    b = j % 2
                    g, par = j % GROUPS, j // GROUPS
                    if g == 0 and not last:
                        act.wait_ge(xT_done, T + par + 1)
                        A(XT[:, par, :], VPS[:, 256:384], ACT.Copy).then_inc(xT_ready, 1)
                    if active(j, LAG_AV, first, last):
                        s = j - LAG_AV
                        act.wait_ge(av_done, S + (s + 1))
                        if not (first and s < 2):
                            act.wait_ge(wo_done, S + (s - 1))
                        A(OT[:, s % 2, :, :], AVP[:, 0:2 * P].rearrange("p (a b) -> p a b", a=2), ACT.Copy).then_inc(outT_ready, 1)
                    if active(j, LAG_T, first, last):
                        s = j - LAG_T
                        sg, spar = s % GROUPS, (s // GROUPS) % 2
                        act.wait_ge(rotT_done, S + (s + 1))
                        if not (first and s < 2):
                            act.wait_ge(scores_done, S + (s - 1))
                        A(QT[:, s % 2, :, :], TPS_[:, 0:2 * P].rearrange("p (a b) -> p a b", a=2), ACT.Copy)
                        kps = TPS_[:, 2 * P:4 * P].rearrange("p (a b) -> p a b", a=2)
                        if spar:
                            A(KT[:, sg * 2:sg * 2 + 2, 0:WIN], kps[:, :, P - WIN:P], ACT.Copy, scale=KEEP[:, bass.ds(p + (s // UNROLL), 1)])
                        A(KT[:, sg * 2:sg * 2 + 2, WIN + spar * P:WIN + (spar + 1) * P], kps, ACT.Copy).then_inc(qkT_ready, 1)
                    if active(j, LAG_S, first, last):
                        s = j - LAG_S
                        act.wait_ge(bias_ready, S + (s + 1))
                        if not (first and s < 2):
                            act.wait_ge(probsT_done, S + (s - 1))
                            act.wait_ge(prevT_ready, S + (s - 1))
                        for i in range(GH):
                            hh, pr = i // 2, i % 2
                            e = A(PR[:, s % 2, i, :], SP2[hh][:, pr * SPAN:(pr + 1) * SPAN], ACT.Exp, bias=BIAS[:, s % 2, i:i + 1],
                                  scale=RN[:, s % UNROLL, 2 * pr + hh:2 * pr + hh + 1], accum_out=SUM[:, s % 2, i:i + 1])
                        e.then_inc(exp_done, 1)
                    if not last:
                        act.wait_ge(qkv_done, S + j + 1)
                        if not (first and j < 2):
                            act.wait_ge(summed, S + (j - 1))
                        A(SQ[:, b, :], QKP[:, :], ACT.Square).then_inc(squared, 1)
                        if not (first and j < UNROLL):
                            act.wait_ge(av_done, S + (j - UNROLL + 1))
                            act.wait_ge(vtail_ready, S + (j - UNROLL + 1))
                        A(V[:, par, g * GW:(g + 1) * GW], VPS[:, 0:GW], ACT.Copy).then_inc(v_ready, 1)

            def ffn(L):
                C, C3 = act.snap(L * CHUNKS), act.snap(L * (3 * CHUNKS))
                act.wait_ge(lvec_ready, act.snap(L * 3 + 3))
                for c in range(CHUNKS):
                    act.wait_ge(xnT_done, C + (c + 1))
                    if c >= 2:
                        act.wait_ge(w1_done, C3 + 3 * (c - 1))
                    A(XNT[:, c % 2, :], XNP[:, :], ACT.Identity, scale=LVEC[:, 0:1], bias=LVEC[:, 1:2]).then_inc(xnT_ready, 1)
                    for k, (lo, n) in enumerate(HCH):
                        act.wait_ge(w1_done, C3 + (3 * c + k + 1))
                        if c:
                            act.wait_ge(hT_ready, C3 + (3 * (c - 1) + k + 1))
                        A(GL[0:n, k, :], GATE[k][0:n, :], ACT.Gelu, bias=BVEC[0:n, k, 1:2]).then_inc(gelu_ready, 1)

            def global_attention():
                act.wait_ge(waT_done, 1)
                A(WAT[:, :, :], SA[:, 0:3 * P].rearrange("p (a b) -> p a b", a=3), ACT.Copy).then_inc(waT_ready, 1)
                with act.Fori(0, SEQS) as q:
                    G = act.snap(q * TPS)
                    act.wait_ge(g_xT, q + 1)
                    for n in range(2):
                        A(GXT[:, 4 * n:4 * n + 4, :], SP2[n][:, :].rearrange("p (a b) -> p a b", a=4), ACT.Copy).then_inc(g_xTc, 1)
                    act.wait_ge(g_proj, q + 1)
                    for n, bank in enumerate((QKP, VPS)):
                        A(GQT[:, n * 512:(n + 1) * 512], bank[:, :], ACT.Copy).then_inc(g_projc, 1)
                    A(GV[:, 0:4, :], AVP[:, :].rearrange("p (a b) -> p a b", a=4), ACT.Copy).then_inc(g_projc, 1)
                    for i in range(TPS):
                        act.wait_ge(g_max, G + (i + 1))
                        if i >= 2:
                            act.wait_ge(g_pt, G + (i - 1))
                            act.wait_ge(g_rs, G + (i - 1))
                        banks = [[SA, SB_], [QKP, VPS]][i % 2]
                        for n in range(2):
                            e = A(GP[:, i % 2, n * 512:(n + 1) * 512], banks[n][:, :], ACT.Exp, bias=GMX[:, i % 2:i % 2 + 1],
                                  accum_out=BIAS[:, i % 2, n:n + 1])
                        e.then_inc(g_exp, 1)
                        act.wait_ge(g_pt, G + (i + 1))
                        if i >= 2:
                            act.wait_ge(g_av, G + (i - 1))
                        A(GPT[:, i % 2, 0:512], TPS_[:, :], ACT.Copy).then_inc(g_ptc, 1)

            for half in range(2):
                if half == 1:
                    global_attention()
                with act.Fori(0, LAYERS) as l:
                    L = half * LAYERS + l
                    slot_loop(act, L, slots)
                    ffn(L)

        @block.vector
        def _(dve):
            dve.wait_ge(const_in, 16 * (N_CONST + 3))
            dve.tensor_copy(IDB[:, :], IDF[:, :])
            for i in range(2):
                dve.tensor_copy(MASKO[:, i, :], MRAW[:, 1, :])
                for a in range(0, ITERS, TPS // 2):
                    dve.tensor_copy(MASK[:, a + 1:a + TPS // 2, i, :], MRAW[:, 1:2, :].to_broadcast([P, TPS // 2 - 1, SPAN]))
            for i in range(2):
                dve.tensor_copy(MASK[:, 0:ITERS:TPS // 2, i, :], MRAW[:, 0:1, :].to_broadcast([P, 2, SPAN])).then_inc(mask_ready, 1)
            dve.wait_ge(const_ready, 6)

            links = [0, 0]

            def link(ins):
                ins.then_inc(ln_link, 1)
                links[1] += 1
                dve.wait_ge(ln_link, links[0] + links[1])

            def statistics(src):
                for t in range(TILES):
                    stats = dve.bn_stats(ST[:, t, :], src[:, t, :])
                link(stats)
                dve.memset(LT[:, :], 0.0)
                for t in range(TILES):
                    agg = dve.bn_aggr(MV[:, t, :], ST[:, t, :])
                link(agg)
                link(dve.tensor_scalar(LV[:, :], MV[:, :, 1], 1e-5, None, ALU.add))
                link(dve.tensor_scalar(LH[:, :], LV[:, :].bitcast(I32), 1, None, ALU.logical_shift_right))
                link(dve.tensor_scalar(RSTD[:, :].bitcast(I32), LH[:, :], -1, MAGIC, ALU.mult, ALU.add))
                for _ in range(NEWTON):
                    link(dve.scalar_tensor_tensor(LT[:, :], RSTD[:, :], -0.5, RSTD[:, :], ALU.mult, ALU.mult))
                    link(dve.tensor_tensor(LT[:, :], LT[:, :], LV[:, :], ALU.mult))
                    link(dve.scalar_tensor_tensor(RSTD[:, :], LT[:, :], 1.5, RSTD[:, :], ALU.add, ALU.mult))

            STAT_LINKS = 5 + 3 * NEWTON

            def normalize(dst, src, t):
                return dve.tensor_scalar(dst, src, MV[:, t, 0:1], RSTD[:, t:t + 1], ALU.subtract, ALU.mult)

            def enter_stack():
                statistics(XO)
                for c in range(CHUNKS):
                    for t in range(c * CT, (c + 1) * CT):
                        dve.tensor_scalar(XSA[:, t, 0:DH], XO[:, t, 0:DH], MV[:, t, 0:1], RSTD[:, t:t + 1], ALU.subtract, ALU.mult)
                        w = normalize(X[:, t, :], XO[:, t, :], t)
                    w.then_inc(x_chunk, 1)

            def slots(L, U, p, first, last):
                S, T = dve.snap(U * UNROLL), dve.snap(U * 2)
                for j in range(UNROLL):
                    b = j % 2
                    g, par = j % GROUPS, j // GROUPS
                    if active(j, 4, first, last):
                        s = j - 4
                        dve.wait_ge(exp_done, S + (s + 1))
                        dve.reciprocal(RSUM[:, s % 2, :], SUM[:, s % 2, :]).then_inc(recip_done, 1)
                    if active(j, LAG_PT, first, last):
                        s = j - LAG_PT
                        dve.wait_ge(probsT_done, S + (s + 1))
                        if not (first and s < 2):
                            dve.wait_ge(av_done, S + (s - 1))
                        dve.tensor_copy(PT[:, s % 2, :, :], PTPS[:, :].rearrange("p (a b) -> p a b", a=GH)).then_inc(probsT_ready, 1)
                    if active(j, 4, first, last):
                        s = j - 4
                        dve.wait_ge(recip_done, S + (s + 1))
                        pr = PR[:, s % 2, :, :]
                        dve.tensor_tensor(pr, pr, RSUM[:, s % 2, :].unsqueeze(2).to_broadcast([P, GH, SPAN]), ALU.mult).then_inc(probs_ready, 1)
                    if active(j, LAG_S, first, last):
                        s = j - LAG_S
                        sg, spar = s % GROUPS, (s // GROUPS) % 2
                        dve.wait_ge(v_ready, S + (s + 1))
                        if not (first and s < GROUPS):
                            dve.wait_ge(av_done, S + (s - GROUPS + 1))
                        dve.tensor_copy(VP[0:WIN, 1 - spar, sg * GW:(sg + 1) * GW], V[P - WIN:P, spar, sg * GW:(sg + 1) * GW]).then_inc(vtail_ready, 1)
                        dve.wait_ge(scores_done, S + (s + 1))
                        for hh in range(2):
                            mx = dve.tensor_reduce(MX[:, s % 2, 2 * hh:2 * hh + 2], SP2[hh][:, 0:2 * SPAN].rearrange("p (h c) -> p h c", h=2), AX.X, ALU.max)
                        mx.then_inc(max_done, 1)
                    if active(j, 4, first, last):
                        s = j - 4
                        dve.wait_ge(probs_ready, S + (s + 1))
                        if not (first and s < 2):
                            dve.wait_ge(av_done, S + (s - 1))
                        dve.transpose(PTP[0:WIN, s % 2, :, :], PR[0:WIN, s % 2, :, 0:WIN]).then_inc(prevT_ready, 1)
                    if active(j, LAG_S, first, last):
                        s = j - LAG_S
                        dve.wait_ge(max_done, S + (s + 1))
                        dve.wait_ge(rot_ready, S + (s + 1))
                        dve.scalar_tensor_tensor(BIAS[:, s % 2, :].rearrange("p (a b) -> p a b", a=2), MX[:, s % 2, :].rearrange("p (a b) -> p a b", a=2), -1.0,
                                                 RN[:, s % UNROLL, 0:GH].rearrange("p (b a) -> p a b", a=2), ALU.mult, ALU.mult).then_inc(bias_ready, 1)
                    if active(j, LAG_WO, first, last) and (j - LAG_WO) % GROUPS == GROUPS - 1:
                        s = j - LAG_WO
                        tt = p * 2 + (s // GROUPS)
                        dve.wait_ge(wo_done, S + (s + 1))
                        o = WOP[:, 0:P].rearrange("p (a b) -> p a b", a=1)
                        xt = X[:, bass.ds(tt, 1), :]
                        odd = (s // GROUPS) % 2
                        dve.tensor_tensor(XSF[:, bass.ds(tt, 1), 0:DH], o[:, :, 0:DH], xt[:, :, 0:DH], ALU.add).then_inc(half_f, 1)
                        if odd:
                            cp = p + (s // UNROLL)
                            rows = slice(P - WIN, P)
                            dve.tensor_tensor(CARRY[rows, bass.ds(cp, 1), :], o[rows, :, DH:P], X[rows, bass.ds(tt, 1), DH:P], ALU.add).then_inc(carried, 1)
                            dve.wait_ge(carried, dve.snap(U * 2 + ((s // UNROLL) * 2 + 1)))
                            dve.tensor_scalar(CARRY[rows, bass.ds(cp, 1), :], CARRY[rows, bass.ds(cp, 1), :], KEEP[rows, bass.ds(cp, 1)], None, ALU.mult).then_inc(carried, 1)
                        dve.wait_ge(half_f, T + (s // GROUPS + 1))
                        dve.tensor_tensor(xt, o, xt, ALU.add).then_inc(x_tile, 1)
                    if g == 1 and not last:
                        if not (first and par == 0):
                            dve.wait_ge(xT_done, T + par)
                        dve.tensor_scalar(XST[:, 1 - par:2 - par, :], XSA[:, bass.ds(p * 2 + par + 1, 1), :], 1.0, None, ALU.mult).then_inc(xs_staged, 1)
                    if not last:
                        if j == 0:
                            tq = 0 if first else dve.snap((p % (TPS // 2)) * 2)
                        dve.wait_ge(squared, S + j + 1)
                        if not (first and j < 2):
                            dve.wait_ge(rot_added, S + (j - 1))
                        raw = QKP[:, :].rearrange("p (a h d) -> p a h d", a=2, h=GH)
                        qc = QKC[:, b, :].rearrange("p (a h d) -> p a h d", a=2, h=GH)
                        qs = QKS[:, b, :].rearrange("p (a h d) -> p a h d", a=2, h=GH)
                        HF = DH // 2

                        def tab(t, lo, n):
                            v = t[:, bass.ds(tq + par, 1), :].rearrange("p o (a d) -> p (o a) d", a=2)[:, :, lo:lo + n]
                            return v.unsqueeze(2).to_broadcast([P, 2, GH, n])
                        dve.tensor_tensor(qc, raw, tab(TABC, 0, DH), ALU.mult)
                        dve.tensor_tensor(qs[:, :, :, 0:HF], raw[:, :, :, HF:DH], tab(TABS, 0, HF), ALU.mult)
                        dve.tensor_tensor(qs[:, :, :, HF:DH], raw[:, :, :, 0:HF], tab(TABS, HF, HF), ALU.mult).then_inc(rotprod_done, 1)
                        dve.tensor_reduce(SS[:, b, :], SQ[:, b, :].rearrange("p (h d) -> p h d", d=DH), AX.X, ALU.add).then_inc(summed, 1)
                        dve.wait_ge(summed, S + j + 1)
                        if not (first and j < 2):
                            dve.wait_ge(rot_ready, S + (j - 1))
                        dve.tensor_scalar(SSC[:, b, :], SS[:, b, :], 1e-24, None, ALU.max).then_inc(clamped, 1)
                        dve.wait_ge(clamped, S + j + 1)
                        dve.tensor_scalar(SSH[:, b, :], SSC[:, b, :], -0.5, None, ALU.mult)
                        dve.tensor_scalar(HALF[:, b, :], SSC[:, b, :].bitcast(I32), 1, None, ALU.logical_shift_right).then_inc(halved, 1)
                        dve.wait_ge(halved, S + j + 1)
                        dve.tensor_scalar(SEED[:, b, :].bitcast(I32), HALF[:, b, :], -1, MAGIC, ALU.mult, ALU.add).then_inc(seeded, 1)

            def ffn(L, l, half):
                C, C3 = dve.snap(L * CHUNKS), dve.snap(L * (3 * CHUNKS))
                dve.tensor_copy(LVEC[:, 0:1], LNG[:, bass.ds(l, 1)]).then_inc(lvec_ready, 1)
                dve.tensor_copy(LVEC[:, 1:2], LNB[:, bass.ds(l, 1)]).then_inc(lvec_ready, 1)
                dve.tensor_copy(BVEC[:, :, :], B1[:, :, bass.ds(l, 1), :].rearrange("p k a c -> p k (a c)")).then_inc(lvec_ready, 1)
                dve.tensor_copy(B2L[:, :].rearrange("p (a b) -> p a b", a=1), B2[:, bass.ds(l, 1), :])
                for i in range(2):
                    dve.wait_ge(shift_f[i], dve.snap(L * (32 * ITERS) + 32 * ITERS))
                links[0], links[1] = dve.snap(L * STAT_LINKS + (1 + 2 * half) * STAT_LINKS), 0
                statistics(XSF)

                def norm_chunk(c):
                    if c >= 2:
                        dve.wait_ge(xnT_done, C + (c - 1))
                    for i in range(CT):
                        t = c * CT + i
                        n = normalize(XN[:, c % 2, i, :], XSF[:, t, :], t)
                    n.then_inc(xn_ready, 1)

                def update(c):
                    dve.wait_ge(y_done, C + (c + 1))
                    dve.tensor_tensor(YB[:, c % 2, :, :], YP[:, :].rearrange("p (a b) -> p a b", a=CT), B2L[:, :].unsqueeze(1).to_broadcast([P, CT, P]), ALU.add).then_inc(yb_ready, 1)
                    dve.wait_ge(yb_ready, C + (c + 1))
                    tt = slice(c * CT, (c + 1) * CT)
                    dve.tensor_tensor(XSA[:, tt, 0:DH], YB[:, c % 2, :, 0:DH], X[:, tt, 0:DH], ALU.add).then_inc(half_a, 1)
                    dve.wait_ge(half_a, C + (c + 1))
                    dve.tensor_tensor(X[:, tt, :], YB[:, c % 2, :, :], X[:, tt, :], ALU.add).then_inc(x_chunk, 1)

                norm_chunk(0)
                norm_chunk(1)
                for c in range(CHUNKS):
                    if c >= 2:
                        dve.wait_ge(y_done, C + (c - 1))
                    for k, (lo, n) in enumerate(HCH):
                        dve.wait_ge(gelu_ready, C3 + (3 * c + k + 1))
                        dve.scalar_tensor_tensor(HT[0:n, c % 2, k, :], LIN[k][0:n, :], BVEC[0:n, k, 0:1], GL[0:n, k, :], ALU.add, ALU.mult).then_inc(hT_ready, 1)
                    if c + 2 < CHUNKS:
                        norm_chunk(c + 2)
                    if c:
                        update(c - 1)
                update(CHUNKS - 1)

            def leave_stack(n):
                dve.wait_ge(x_chunk, n)
                dve.scalar_tensor_tensor(XO[:, :, :], X[:, :, :], 0.5, XO[:, :, :], ALU.mult, ALU.add).then_inc(outer_done, 1)

            def global_attention():
                with dve.Fori(0, SEQS) as q:
                    G = dve.snap(q * TPS)
                    for i in range(TPS):
                        t = q * TPS + i
                        n = dve.tensor_scalar(GX[:, i:i + 1, :], XO[:, bass.ds(t, 1), :], MV[:, bass.ds(t, 1), 0:1].rearrange("p a b -> p (a b)"),
                                              RSTD[:, bass.ds(t, 1)], ALU.subtract, ALU.mult)
                    n.then_inc(g_xn, 1)
                    dve.wait_ge(g_proj, q + 1)
                    for n, bank in enumerate((TPS_, PTPS)):
                        dve.tensor_copy(GKT[:, n * 512:(n + 1) * 512], bank[:, :]).then_inc(g_projc, 1)
                    dve.tensor_copy(GV[:, 4:8, :], WOP[:, :].rearrange("p (a b) -> p a b", a=4)).then_inc(g_projc, 1)

                    def finish(i):
                        dve.wait_ge(g_av, G + (i + 1))
                        dve.wait_ge(g_rs, G + (i + 1))
                        xt = XO[:, bass.ds(q * TPS + i, 1), :]
                        dve.scalar_tensor_tensor(xt, AVP[:, 0:P].rearrange("p (a b) -> p a b", a=1), GRS[:, i % 2:i % 2 + 1], xt, ALU.mult, ALU.add).then_inc(g_out, 1)

                    for i in range(TPS):
                        dve.wait_ge(g_s, G + (i + 1))
                        banks = [[SA, SB_], [QKP, VPS]][i % 2]
                        for n in range(2):
                            m = dve.tensor_reduce(MX[:, i % 2, n:n + 1], banks[n][:, :], AX.X, ALU.max)
                        m.then_inc(g_link, 1)
                        dve.wait_ge(g_link, dve.snap((G + i) * 4 + 1))
                        if i >= 2:
                            dve.wait_ge(g_exp, G + (i - 1))
                        dve.tensor_tensor(GMX[:, i % 2:i % 2 + 1], MX[:, i % 2, 0:1], MX[:, i % 2, 1:2], ALU.max).then_inc(g_link, 1)
                        dve.wait_ge(g_link, dve.snap((G + i) * 4 + 2))
                        dve.tensor_scalar(GMX[:, i % 2:i % 2 + 1], GMX[:, i % 2:i % 2 + 1], -1.0, None, ALU.mult).then_inc(g_max, 1)
                        dve.wait_ge(g_exp, G + (i + 1))
                        dve.tensor_tensor(GSUM[:, i % 2:i % 2 + 1], BIAS[:, i % 2, 0:1], BIAS[:, i % 2, 1:2], ALU.add).then_inc(g_link, 1)
                        dve.wait_ge(g_link, dve.snap((G + i) * 4 + 3))
                        dve.reciprocal(GRS[:, i % 2:i % 2 + 1], GSUM[:, i % 2:i % 2 + 1]).then_inc(g_link, 1)
                        dve.wait_ge(g_link, dve.snap((G + i) * 4 + 4))
                        dve.tensor_scalar(GRS[:, i % 2:i % 2 + 1], GRS[:, i % 2:i % 2 + 1], NORM, None, ALU.mult).then_inc(g_rs, 1)
                        dve.wait_ge(g_pt, G + (i + 1))
                        if i >= 2:
                            dve.wait_ge(g_av, G + (i - 1))
                        dve.tensor_copy(GPT[:, i % 2, 512:1024], PTPS[:, :]).then_inc(g_ptc, 1)
                        finish(i)

            enter_stack()
            for half in range(2):
                if half == 1:
                    links[0], links[1] = 0, (LAYERS + 1) * STAT_LINKS
                    dve.wait_ge(outer_done, 1)
                    statistics(XO)
                    global_attention()
                    dve.wait_ge(g_out, TILES)
                    dve.tensor_copy(LT[:, 0:1], ROPEC[:, 0, 0:1]).then_inc(outer_done, 1)
                    for c in range(2):
                        dve.wait_ge(shift_a[c], (LAYERS + 1) * 16 * CHUNKS)
                    enter_stack()
                with dve.Fori(0, LAYERS) as l:
                    L = half * LAYERS + l
                    for c in range(2):
                        dve.wait_ge(shift_a[c], dve.snap((half * (LAYERS + 1) + 1 + l) * (16 * CHUNKS)))
                    dve.tensor_scalar(XST[:, 0, :], XSA[:, 0, :], 1.0, None, ALU.mult).then_inc(xs_staged, 1)
                    dve.wait_ge(tab_ready, dve.snap(L * 2 + 2))
                    slot_loop(dve, L, slots)
                    ffn(L, l, half)
                leave_stack((half + 1) * (LAYERS + 1) * CHUNKS)


def rotary_constants():
    f = np.float32
    half = np.arange(0, DH, 2, dtype=f)
    inv_freq = (f(1.0) / f(10000.0) ** (half / f(DH))).astype(f)
    t = np.arange(SEQ, dtype=f)
    freqs = t[:, None] * inv_freq[None, :]
    base = (half + f(0.4 * DH)) / f(1.4 * DH)
    scale = base[None, :] ** ((t - f(SEQ // 2)) / f(WIN // 2))[:, None]
    cos, sin = np.cos(freqs), np.sin(freqs)
    sign_sin = np.concatenate([-sin, sin], -1)
    cos, scale = np.concatenate([cos, cos], -1), np.concatenate([scale, scale], -1)
    c = np.concatenate([8 * cos * scale, cos * (1 / scale)], -1)
    s = np.concatenate([8 * sign_sin * scale, sign_sin * (1 / scale)], -1)
    return [np.ascontiguousarray(a.astype(f).reshape(TPS, P, P).transpose(1, 0, 2)) for a in (c, s)]


def mask_constants():
    i, key = np.arange(P)[:, None], np.arange(SPAN)[None, :] - WIN
    seen = (i >= key) & (i - key <= WIN)
    both = np.stack([seen & (key >= 0), seen], 1)
    return np.where(both, 0.0, NEG).astype(np.float32)


def kernel(**inputs):
    import concourse.bacc as bacc
    from concourse.bass_utils import run_bass_kernel_spmd

    i = {k: np.asarray(v) for k, v in inputs.items()}
    swap = np.concatenate([np.arange(DH // 2, DH), np.arange(DH // 2)])
    cos, sin = rotary_constants()
    qs, ks = i["L0_ffn_q_scale"], i["L0_ffn_k_scale"]
    arrays = {
        "x": i["L0_attn_x"], "wq": i["L0_attn_Wq"], "wk": i["L0_attn_Wk"], "wv": i["L0_attn_Wv"],
        "wqkv": i["L0_ffn_Wqkv"],
        "qk_rows": np.concatenate([qs, ks], 1), "qk_swap_rows": np.concatenate([qs[:, swap], ks[:, swap]], 1),
        "wo": i["L0_ffn_Wo"], "ln_g": i["L0_ffn_ln_g"].T, "ln_b": i["L0_ffn_ln_b"].T, "w1": i["L0_ffn_W1"],
        "b1": i["L0_ffn_b1"].reshape(LAYERS, 2, HID).transpose(2, 0, 1), "w2": i["L0_ffn_W2"], "b2": i["L0_ffn_b2"],
        "rope_cos": cos, "rope_sin": sin, "ident": np.eye(P, dtype=np.float32), "masks": mask_constants(),
    }
    arrays = {k: np.ascontiguousarray(v) for k, v in arrays.items()}
    nc = bacc.Bacc("TRN2", target_bir_lowering=False, num_devices=1)
    args = [nc.dram_tensor(k, v.shape, F32, kind="ExternalInput").ap() for k, v in arrays.items()]
    out = nc.dram_tensor("y", (SEQS, SEQ, P), F32, kind="ExternalOutput").ap()
    build(nc, *args, out)
    r = run_bass_kernel_spmd(nc, [arrays], core_ids=[0])
    return r.results[0]["y"]
```

```python
import math
from contextlib import ExitStack

import numpy as np

import concourse.bass as bass
from concourse import mybir

F32 = mybir.dt.float32
BF16 = mybir.dt.bfloat16
F32R = mybir.dt.float32r
I32 = mybir.dt.int32
ALU = mybir.AluOpType
ACT = mybir.ActivationFunctionType
AX = mybir.AxisListType

P = 128
SEQS, SEQ = 2, 1024
TPS = SEQ // P
TILES = SEQS * TPS
LAYERS = 6
HEADS, DH, WIN = 16, 64, 32
INNER = HEADS * DH
GH = 4
GROUPS = HEADS // GH
PAIRS = HEADS // 2
GW = GH * DH
SPAN = WIN + P
UNROLL = 2 * GROUPS
ITERS = TILES // 2
SLOTS = TILES * GROUPS
HID = 341
HCH = [(0, 128), (128, 128), (256, HID - 256)]
CT = 4
CHUNKS = TILES // CT
LAG_T, LAG_S, LAG_EXP, LAG_PT, LAG_AV, LAG_WO = 3, 4, 5, 6, 7, 8
LAG_TAIL = 5
NEG = -1.0e30
MAGIC = 0x5F3759DF
NEWTON = 3
RN_STEPS = 2 + 3 * NEWTON
NORM = 1.0 / math.sqrt(128.0)


def build(nc, x, wq, wk, wv, wqkv, qk_rows, qk_swap_rows, wo, ln_g, ln_b, w1, b1, w2, b2,
          rope_cos, rope_sin, ident, masks, out):
    with ExitStack() as ctx:
        def sb(name, shape, dt=F32):
            return ctx.enter_context(nc.sbuf_tensor(name, shape, dt))

        def ps(name):
            return ctx.enter_context(nc.psum_tensor(name, [P, 512], F32))

        def sem(name):
            return ctx.enter_context(nc.semaphore(name))

        X = sb("X", [P, TILES, P])
        XO = sb("XO", [P, TILES, P])
        XSA = sb("XSA", [P, TILES + 1, P])
        XSF = sb("XSF", [P, TILES + 1, P])
        IDF = sb("IDF", [P, P])
        IDB = sb("IDB", [P, P], BF16)
        MRAW = sb("MRAW", [P, 2, SPAN])
        MASK = sb("MASK", [P, ITERS, 2, SPAN], BF16)
        MASKO = sb("MASKO", [P, 2, SPAN], BF16)
        ROPEC = sb("ROPEC", [P, TPS, P])
        ROPES = sb("ROPES", [P, TPS, P])
        TABC = sb("TABC", [P, TPS, P])
        TABS = sb("TABS", [P, TPS, P])
        QKSC = sb("QKSC", [P, LAYERS, P])
        QKSW = sb("QKSW", [P, LAYERS, P])
        LNG = sb("LNG", [P, LAYERS])
        LNB = sb("LNB", [P, LAYERS])
        B1 = sb("B1", [P, 3, LAYERS, 2])
        B2 = sb("B2", [P, LAYERS, P])
        WQH = sb("WQH", [P, GROUPS, 3 * GW], F32R)
        WQL = sb("WQL", [P, GROUPS, 3 * GW], F32R)
        WO = sb("WO", [P, PAIRS, P])
        W1 = sb("W1", [P, 2 * HID])
        W2 = sb("W2", [P, 3, P])
        WA = sb("WA", [P, 3, P])
        WAT = sb("WAT", [P, 3, P])
        KEEP = sb("KEEP", [P, ITERS])
        CARRY = sb("CARRY", [P, ITERS, DH])
        LVEC = sb("LVEC", [P, 2])
        BVEC = sb("BVEC", [P, 3, 2])
        B2L = sb("B2L", [P, P])
        XST = sb("XST", [P, 2, P])
        XTH = sb("XTH", [P, 2, P], F32R)
        XTL = sb("XTL", [P, 2, P], F32R)
        SQ = sb("SQ", [P, 2, 2 * GW])
        SS = sb("SS", [P, 2, 2 * GH])
        SSC = sb("SSC", [P, 2, 2 * GH])
        NT = sb("NT", [P, 2 * GH])
        RN = sb("RN", [P, UNROLL, 2 * GH])
        QKC = sb("QKC", [P, 2, 2 * GW])
        QKS = sb("QKS", [P, 2, 2 * GW])
        WRAW = [SQ, QKC, QKS]
        QKR = sb("QKR", [P, 4, 2 * GW])
        QT = sb("QT", [P, 2, 2, P])
        KT = sb("KT", [P, PAIRS, WIN + 2 * P])
        V = sb("V", [P, 2, INNER])
        VP = sb("VP", [WIN, 2, INNER])
        MX = sb("MX", [P, 2, GH])
        BIAS = sb("BIAS", [P, 2, GH])
        SUM = sb("SUM", [P, 2, GH])
        RSUM = sb("RSUM", [P, 2, GH])
        PR = sb("PR", [P, 4, GH, SPAN])
        PT = sb("PT", [P, 2, GH, P])
        PTP = sb("PTP", [WIN, 2, GH, WIN])
        OT = sb("OT", [P, 2, 2, P])
        ST = sb("ST", [P, TILES, 6])
        MV = sb("MV", [P, TILES, 2])
        LV = sb("LV", [P, TILES])
        LT = sb("LT", [P, TILES])
        RSTD = sb("RSTD", [P, TILES])
        XN = sb("XN", [P, 2, CT, P])
        XNT = sb("XNT", [P, 2, CT * P])
        GL = sb("GL", [P, 3, CT * P])
        HT = sb("HT", [P, 2, 3, CT * P])
        YB = sb("YB", [P, 2, CT, P])
        GXT = TABC
        GQT = XNT[:, :, :].rearrange("p a b -> p (a b)")
        GKT = YB[:, :, :, :].rearrange("p a b c -> p (a b c)")
        GV = XN[:, :, :, :].rearrange("p a b c -> p (a b) c")
        GX = TABS
        GP = V
        GPT = HT[:, :, :, :].rearrange("p a b c -> p (a b c)")[:, 0:2 * SEQ].rearrange("p (a b) -> p a b", a=2)
        GMX = sb("GMX", [P, 2])
        GSUM = sb("GSUM", [P, 2])
        GRS = sb("GRS", [P, 2])

        QKP, VPS, TPS_, SA, SB_, PTPS, AVP, WOP = [ps(n) for n in ("b_qk", "b_v", "b_t", "b_sa", "b_sb", "b_pt", "b_av", "b_wo")]
        SP2 = [SA, SB_]
        XNP, YP = QKP, WOP
        GATE, LIN = [VPS, TPS_, SA], [SB_, PTPS, AVP]

        x_in = sem("x_in")
        const_in = sem("const_in")
        late_in = sem("late_in")
        const_ready = sem("const_ready")
        mask_ready = sem("mask_ready")
        b1_cleared = sem("b1_cleared")
        wqkv_in = sem("wqkv_in")
        ffw_in = sem("ffw_in")
        lvec_ready = sem("lvec_ready")
        wq_high = sem("wq_high"); wq_split = sem("wq_split")
        tab_ready = sem("tab_ready")
        qk_done = sem("qk_done"); qkv_done = sem("qkv_done"); rotT_done = sem("rotT_done"); scores_done = sem("scores_done")
        probsT_done = sem("probsT_done"); av_done = sem("av_done"); wo_done = sem("wo_done")
        squared = sem("squared"); v_ready = sem("v_ready"); qkT_ready = sem("qkT_ready")
        exp_done = sem("exp_done"); outT_ready = sem("outT_ready")
        rotprod_done = sem("rotprod_done"); summed = sem("summed"); rn_step = sem("rn_step"); max_done = sem("max_done"); bias_ready = sem("bias_ready")
        recip_done = sem("recip_done"); probs_ready = sem("probs_ready"); prevT_ready = sem("prevT_ready")
        probsT_ready = sem("probsT_ready"); vtail_ready = sem("vtail_ready")
        rot_added = sem("rot_added"); rot_ready = sem("rot_ready")
        xs_staged = sem("xs_staged"); xT_done = sem("xT_done"); xT_high = sem("xT_high"); xT_low = sem("xT_low")
        x_tile = sem("x_tile")
        shift_f = [sem(f"shift_f{i}") for i in range(2)]
        x_chunk = sem("x_chunk"); xn_ready = sem("xn_ready"); xnT_done = sem("xnT_done"); xnT_ready = sem("xnT_ready")
        y_done = sem("y_done"); yb_ready = sem("yb_ready")
        shift_a = [sem(f"shift_a{i}") for i in range(2)]
        w1_done = sem("w1_done"); gelu_ready = sem("gelu_ready"); hT_ready = sem("hT_ready")
        ln_link = sem("ln_link")
        carried = sem("carried"); half_f = sem("half_f"); half_a = sem("half_a")
        g_link = sem("g_link")
        outer_done = sem("outer_done")
        out_done = sem("out_done")
        waT_done = sem("waT_done"); waT_ready = sem("waT_ready"); g_xn = sem("g_xn"); g_xT = sem("g_xT"); g_xTc = sem("g_xTc")
        g_proj = sem("g_proj"); g_projc = sem("g_projc"); g_s = sem("g_s"); g_max = sem("g_max"); g_exp = sem("g_exp")
        g_pt = sem("g_pt"); g_ptc = sem("g_ptc"); g_av = sem("g_av"); g_rs = sem("g_rs"); g_out = sem("g_out")

        block = ctx.enter_context(nc.Block())
        N_CONST = 6
        N_LATE = 9

        def tile_of(p, j):
            return p * 2 + j // GROUPS

        def slot_loop(e, L, half, slots):
            slots(L, half, e.snap(L * ITERS), 0, True, False)
            with e.Fori(1, ITERS) as p:
                slots(L, half, e.snap(L * ITERS + p), p, False, False)
            slots(L, half, e.snap(L * ITERS + ITERS), ITERS, False, True)

        def active(j, lag, first, last):
            return not (first and j < lag) and not (last and j >= lag)

        @block.sync
        def _(sp):
            sp.dma_start(XO[:, :, :], x.rearrange("b (t p) d -> p (b t) d", p=P)).then_inc(x_in, 16)

            def load_attention_weights(layer):
                src = wqkv[bass.ds(layer, 1), :, :].rearrange("a e n -> (a e) n")
                for part in range(3):
                    sp.dma_start(WRAW[part][:, :, :].rearrange("p a b -> p (a b)"), src[:, part * INNER:(part + 1) * INNER]).then_inc(wqkv_in, 16)
                sp.dma_start(WO[:, :, :], wo[bass.ds(layer, 1), :, :].rearrange("a (q p) n -> p (a q) n", p=P)).then_inc(wqkv_in, 16)

            def plain_wait():
                sp.wait_ge(x_in, 16)

            sp.dma_start(IDF[:, :], ident).then_inc(const_in, 16)
            load_attention_weights(0)
            sp.dma_start(ROPEC[:, :, :], rope_cos).then_inc(const_in, 16)
            sp.dma_start(ROPES[:, :, :], rope_sin).then_inc(const_in, 16)
            sp.dma_start(QKSC[:, :, :], qk_rows.partition_broadcast(P)).then_inc(const_in, 16)
            sp.dma_start(QKSW[:, :, :], qk_swap_rows.partition_broadcast(P)).then_inc(const_in, 16)
            sp.dma_start(MRAW[:, :, :], masks).then_inc(const_in, 16)

            def load_late():
                sp.dma_start(B2[:, :, :], b2.partition_broadcast(P)).then_inc(late_in, 16)
                sp.dma_start(LNG[:, :], ln_g).then_inc(late_in, 16)
                sp.dma_start(LNB[:, :], ln_b).then_inc(late_in, 16)
                sp.wait_ge(b1_cleared, 1)
                for k, (lo, n) in enumerate(HCH):
                    sp.dma_start(B1[0:n, k, :, :], b1[lo:lo + n]).then_inc(late_in, 16)
                for i, w in enumerate((wq, wk, wv)):
                    sp.dma_start(WA[:, i, :], w).then_inc(late_in, 16)

            def shift_chunk(c, seen):
                sp.wait_ge(x_chunk, seen)
                plain_wait()
                t = c * CT
                sp.dma_start(XSA[1:P, t:t + CT, DH:P], X[0:P - 1, t:t + CT, DH:P]).then_inc(shift_a[c % 2], 16)
                n = CT - 1 if (t + CT) % TPS == 0 else CT
                sp.dma_start(XSA[0:1, t + 1:t + 1 + n, DH:P], X[P - 1:P, t:t + n, DH:P]).then_inc(shift_a[c % 2], 16)

            for half in range(2):
                for c in range(CHUNKS):
                    n = half * (LAYERS + 1) * CHUNKS + c
                    shift_chunk(c, n + 1)
                if half == 0:
                    load_late()
                with sp.Fori(0, LAYERS) as l:
                    L = half * LAYERS + l
                    sp.wait_ge(x_chunk, sp.snap((half * (LAYERS + 1) + 1 + l) * CHUNKS))
                    plain_wait()
                    sp.dma_start(W1[:, :], w1[bass.ds(l, 1), :, :].rearrange("a e n -> (a e) n")).then_inc(ffw_in, 16)
                    w2l = w2[bass.ds(l, 1), :, :].rearrange("a h n -> (a h) n")
                    sp.dma_start(W2[:, 0:2, :], w2l[0:2 * P, :].rearrange("(k p) n -> p k n", p=P)).then_inc(ffw_in, 16)
                    sp.dma_start(W2[0:HID - 2 * P, 2, :], w2l[2 * P:HID, :]).then_inc(ffw_in, 16)
                    with sp.Fori(0, ITERS) as p:
                        for jt in range(2):
                            t = p * 2 + jt
                            sp.wait_ge(x_tile, sp.snap(L * TILES + p * 2 + jt + 2))
                            plain_wait()
                            sp.dma_start(XSF[1:P, bass.ds(t, 1), DH:P], X[0:P - 1, bass.ds(t, 1), DH:P]).then_inc(shift_f[jt], 16)
                            last_row = X[P - 1:P, bass.ds(t, 1), DH:P] if jt == 0 else CARRY[P - 1:P, bass.ds(p, 1), :]
                            sp.dma_start(XSF[0:1, bass.ds(t + 1, 1), DH:P], last_row).then_inc(shift_f[jt], 16)
                    sp.wait_ge(wo_done, sp.snap(L * SLOTS + SLOTS + 1))
                    plain_wait()
                    load_attention_weights((l + 1) % LAYERS)
                    for c in range(CHUNKS):
                        n = half * (LAYERS + 1) * CHUNKS + CHUNKS + c
                        shift_chunk(c, sp.snap(l * CHUNKS + (n + 1)))
            sp.wait_ge(outer_done, 3)
            sp.dma_start(out.rearrange("b (t p) d -> p (b t) d", p=P), XO[:, :, :]).then_inc(out_done, 16)
            for c in range(2):
                sp.wait_ge(shift_a[c], 16 * CHUNKS * 2 * (LAYERS + 1))
            sp.wait_ge(wqkv_in, 64 * (2 * LAYERS + 1))
            sp.wait_ge(out_done, 16)

        @block.gpsimd
        def _(pool):
            pool.memset(B1[:, :, :, :], 0.0).then_inc(b1_cleared, 1)
            pool.memset(KEEP[:, :], 1.0).then_inc(const_ready, 1)
            pool.memset(XSA[:, :, :], 0.0).then_inc(const_ready, 1)
            pool.memset(XSF[:, :, :], 0.0).then_inc(const_ready, 1)
            pool.memset(KT[:, :, :], 0.0).then_inc(const_ready, 1)
            pool.memset(VP[:, :, :], 0.0).then_inc(const_ready, 1)
            pool.wait_ge(const_ready, 1)
            pool.memset(KEEP[:, TPS // 2 - 1:ITERS:TPS // 2], 0.0).then_inc(const_ready, 1)
            pool.wait_ge(const_in, 16 * N_CONST)
            pool.wait_ge(const_ready, 6)

            def split_weights(layers):
                pool.wait_ge(wqkv_in, pool.snap(layers * 64 + 64))
                for part, raw in enumerate(WRAW):
                    raw = raw[:, :, :].rearrange("p a b -> p (a b)").rearrange("p (g c) -> p g c", g=GROUPS)
                    hi, lo = [w[:, :, part * GW:(part + 1) * GW] for w in (WQH, WQL)]
                    pool.tensor_tensor(hi, raw, KEEP[:, 0:1].unsqueeze(2).to_broadcast([P, GROUPS, GW]), ALU.mult).then_inc(wq_high, 1)
                    pool.wait_ge(wq_high, pool.snap(layers * 3 + (part + 1)))
                    pool.tensor_tensor(lo, raw, hi, ALU.subtract).then_inc(wq_split, 1)

            def slots(L, half, U, p, first, last):
                S, T = pool.snap(U * UNROLL), pool.snap(U * 2)
                for j in range(UNROLL):
                    if active(j, LAG_EXP, first, last):
                        s = j - LAG_EXP
                        pool.wait_ge(recip_done, S + (s + 1))
                        pr = PR[:, s % 4, :, :]
                        pool.tensor_tensor(pr, pr, RSUM[:, s % 2, :].unsqueeze(2).to_broadcast([P, GH, SPAN]), ALU.mult).then_inc(probs_ready, 1)
                    if not last:
                        pool.wait_ge(rotprod_done, S + j + 1)
                        if not (first and j < 4):
                            pool.wait_ge(rotT_done, S + (j - 3))
                        pool.tensor_tensor(QKR[:, j % 4, :], QKC[:, j % 2, :], QKS[:, j % 2, :], ALU.add).then_inc(rot_added, 1)
                    if active(j, 1, first, last):
                        s = j - 1
                        pool.wait_ge(rn_step, pool.snap(S * RN_STEPS + (s + 1) * RN_STEPS))
                        pool.wait_ge(rot_added, S + (s + 1))
                        kk = QKR[:, s % 4, GW:].rearrange("p (h d) -> p h d", h=GH)
                        pool.tensor_tensor(kk, kk, RN[:, s % UNROLL, GH:].unsqueeze(2).to_broadcast([P, GH, DH]), ALU.mult).then_inc(rot_ready, 1)

            for half in range(2):
                with pool.Fori(0, LAYERS) as l:
                    L = half * LAYERS + l
                    split_weights(L)
                    if half == 1:
                        pool.wait_ge(outer_done, 2)
                    for tab, rope, sc in ((TABC, ROPEC, QKSC), (TABS, ROPES, QKSW)):
                        pool.tensor_tensor(tab[:, :, :], rope[:, :, :], sc[:, bass.ds(l, 1), :].to_broadcast([P, TPS, P]), ALU.mult).then_inc(tab_ready, 1)
                    slot_loop(pool, L, half, slots)

        @block.tensor
        def _(pe):
            pe.wait_ge(const_in, 16 * N_CONST)
            pe.wait_ge(const_ready, 6)
            mm = nc.tensor.matmul

            def to_features(L, c):
                pe.wait_ge(xn_ready, pe.snap(L * CHUNKS + (c + 1)))
                if c:
                    pe.wait_ge(xnT_ready, pe.snap(L * CHUNKS + c))
                for i in range(CT):
                    t = nc.tensor.transpose(XNP[:, i * P:(i + 1) * P], XN[:, c % 2, i, :], IDF[:, :])
                t.then_inc(xnT_done, 1)

            def by_parts(bank, g, par, lo, hi):
                mm(bank, XTH[:, par, :], WQH[:, g, lo:hi], start=True, stop=False)
                mm(bank, XTH[:, par, :], WQL[:, g, lo:hi], start=False, stop=False)
                return mm(bank, XTL[:, par, :], WQH[:, g, lo:hi], start=False, stop=True)

            def first_tile(count):
                pe.wait_ge(xs_staged, count)
                nc.tensor.transpose(VPS[:, 256:384], XST[:, 0, :], IDF[:, :]).then_inc(xT_done, 1)

            def slots(L, half, U, p, first, last):
                S, T = pe.snap(U * UNROLL), pe.snap(U * 2)
                S2 = pe.snap(S * 2)
                XB = pe.snap(T + L + half)
                for j in range(UNROLL):
                    b = j % 2
                    g, par = j % GROUPS, j // GROUPS
                    if not last:
                        if g == 0:
                            pe.wait_ge(xT_low, XB + par + 1)
                        if not (first and j < 1):
                            pe.wait_ge(rotprod_done, S + j)
                        by_parts(QKP[:, :], g, par, 0, 2 * GW).then_inc(qk_done, 1)
                        if not (first and j < 1):
                            pe.wait_ge(v_ready, S + j)
                        by_parts(VPS[:, 0:GW], g, par, 2 * GW, 3 * GW).then_inc(qkv_done, 1)
                    if active(j, LAG_AV, first, last):
                        s = j - LAG_AV
                        q, sg, spar = s % 2, s % GROUPS, (s // GROUPS) % 2
                        pe.wait_ge(probsT_ready, S + (s + 1))
                        pe.wait_ge(prevT_ready, S + (s + 1))
                        if g == GROUPS - 1 and not last:
                            pe.wait_ge(xT_low, XB + par + 2)
                        for i in range(GH):
                            hh, pr = i % 2, i // 2
                            col = sg * GW + i * DH
                            mm(AVP[DH * hh:DH * hh + DH, pr * P:(pr + 1) * P], V[:, spar, col:col + DH], PT[:, q, hh * 2 + pr, :],
                               start=(pr == 0), stop=False, skip_group_check=True)
                        for i in range(GH):
                            hh, pr = i % 2, i // 2
                            col = sg * GW + i * DH
                            last_av = mm(AVP[DH * hh:DH * hh + DH, pr * P:pr * P + WIN], VP[0:WIN, spar, col:col + DH], PTP[0:WIN, q, hh * 2 + pr, :],
                                         start=False, stop=True, skip_group_check=True)
                        last_av.then_inc(av_done, 1)
                    if g == GROUPS - 2 and not last:
                        pe.wait_ge(xs_staged, XB + par + 2)
                        nc.tensor.transpose(AVP[:, 256:384], XST[:, 1 - par, :], IDF[:, :]).then_inc(xT_done, 1)
                    if active(j, LAG_PT, first, last):
                        s = j - LAG_PT
                        pe.wait_ge(probs_ready, S + (s + 1))
                        for i in range(GH):
                            last_pt = nc.tensor.transpose(PTPS[:, i * P:(i + 1) * P], PR[:, s % 4, i, WIN:SPAN], IDF[:, :])
                        last_pt.then_inc(probsT_done, 1)
                    if active(j, LAG_T, first, last):
                        s = j - LAG_T
                        pe.wait_ge(rot_ready, S + (s + 1))
                        if not (first and s < 1):
                            pe.wait_ge(qkT_ready, S + s)
                        for i in range(4):
                            last_t = nc.tensor.transpose(TPS_[:, i * P:(i + 1) * P], QKR[:, s % 4, i * P:(i + 1) * P], IDF[:, :])
                        last_t.then_inc(rotT_done, 1)
                    if active(j, LAG_S, first, last):
                        s = j - LAG_S
                        sg, spar = s % GROUPS, (s // GROUPS) % 2
                        if not active(j, LAG_T, first, last):
                            pe.wait_ge(qkT_ready, S + (s + 1))
                        if spar:
                            m = MASKO[:, :, :]
                        else:
                            m = MASK[:, bass.ds(p + (s // UNROLL), 1), :, :].rearrange("p a h c -> p (a h) c")
                        for hh in range(2):
                            if not (first and s < 1):
                                pe.wait_ge(exp_done, S2 + (2 * s - 1 + hh))
                            mm(SP2[hh][:, 0:2 * SPAN], IDB[:, :], m.rearrange("p h c -> p (h c)"), start=True, stop=False, skip_group_check=True)
                            for pr in range(2):
                                last_s = mm(SP2[hh][:, pr * SPAN:(pr + 1) * SPAN], QT[DH * hh:DH * hh + DH, s % 2, pr, :],
                                            KT[DH * hh:DH * hh + DH, sg * 2 + pr, spar * P:spar * P + SPAN],
                                            start=False, stop=True, skip_group_check=True)
                            last_s.then_inc(scores_done, 1)
                    if last and j == LAG_PT:
                        to_features(L, 0)
                    if active(j, LAG_WO, first, last):
                        s = j - LAG_WO
                        sg = s % GROUPS
                        if not active(j, LAG_AV, first, last):
                            pe.wait_ge(outT_ready, S + (s + 1))
                        if sg == 0 and not (first and s < GROUPS):
                            pe.wait_ge(x_tile, T + (s // GROUPS + 1))
                        for pr in range(2):
                            last_wo = mm(WOP[:, 0:P], OT[:, s % 2, pr, :], WO[:, sg * 2 + pr, :],
                                         start=(sg == 0 and pr == 0), stop=(sg == GROUPS - 1 and pr == 1), skip_group_check=True)
                        last_wo.then_inc(wo_done, 1)

            def ffn(L, half):
                C, C3 = pe.snap(L * CHUNKS), pe.snap(L * (3 * CHUNKS))
                pe.wait_ge(ffw_in, pe.snap(L * 48 + 48))

                def up(c):
                    pe.wait_ge(xnT_ready, C + (c + 1))
                    for k, (lo, n) in enumerate(HCH):
                        if c:
                            pe.wait_ge(hT_ready, C3 + (3 * (c - 1) + k + 1))
                        mm(GATE[k][0:n, :], W1[:, HID + lo:HID + lo + n], XNT[:, c % 2, :], start=True, stop=True)
                        mm(LIN[k][0:n, :], W1[:, lo:lo + n], XNT[:, c % 2, :], start=True, stop=True).then_inc(w1_done, 1)

                def down(c):
                    pe.wait_ge(hT_ready, C3 + (3 * c + 3))
                    if c:
                        pe.wait_ge(yb_ready, C + c)
                    for i in range(CT):
                        for k, (lo, n) in enumerate(HCH):
                            y = mm(YP[:, i * P:(i + 1) * P], HT[0:n, c % 2, k, i * P:(i + 1) * P], W2[0:n, k, :],
                                   start=(k == 0), stop=(k == 2))
                    y.then_inc(y_done, 1)

                for c in range(CHUNKS):
                    up(c)
                    if c + 1 < CHUNKS:
                        to_features(L, c + 1)
                    if c:
                        down(c - 1)
                pe.wait_ge(hT_ready, C3 + (3 * CHUNKS - 2))
                first_tile(pe.snap(L * (TILES + 1) + (TILES + 2 + half)))
                down(CHUNKS - 1)

            def global_attention():
                for i in range(3):
                    t = nc.tensor.transpose(SA[:, i * P:(i + 1) * P], WA[:, i, :], IDF[:, :])
                t.then_inc(waT_done, 1)
                pe.wait_ge(waT_ready, 1)
                with pe.Fori(0, SEQS) as q:
                    G = pe.snap(q * TPS)
                    pe.wait_ge(g_xn, q + 1)
                    for i in range(TPS):
                        t = nc.tensor.transpose(SP2[i // 4][:, (i % 4) * P:(i % 4 + 1) * P], GX[:, i, :], IDF[:, :])
                    t.then_inc(g_xT, 1)
                    pe.wait_ge(g_xTc, q * 2 + 2)
                    for i in range(2):
                        for n in range(2):
                            t = mm([QKP, VPS, TPS_, PTPS][2 * i + n][:, :], WAT[:, i, :], GXT[:, 4 * n:4 * n + 4, :].rearrange("p a b -> p (a b)"), start=True, stop=True)
                    for i in range(TPS):
                        t = mm([AVP, WOP][i // 4][:, (i % 4) * P:(i % 4 + 1) * P], GXT[:, i, :], WAT[:, 2, :], start=True, stop=True)
                    t.then_inc(g_proj, 1)
                    pe.wait_ge(g_projc, q * 6 + 6)

                    def scores(i):
                        for n in range(2):
                            t = mm([[SA, SB_], [QKP, VPS]][i % 2][n][:, :], GQT[:, i * P:(i + 1) * P], GKT[:, n * 512:(n + 1) * 512], start=True, stop=True)
                        t.then_inc(g_s, 1)

                    scores(0)
                    for i in range(TPS):
                        if i + 1 < TPS:
                            if i >= 1:
                                pe.wait_ge(g_exp, G + i)
                            scores(i + 1)
                        pe.wait_ge(g_exp, G + (i + 1))
                        if i:
                            pe.wait_ge(g_ptc, pe.snap(q * (2 * TPS) + 2 * i))
                        for k in range(TPS):
                            t = nc.tensor.transpose([TPS_, PTPS][k // 4][:, (k % 4) * P:(k % 4 + 1) * P], GP[:, i % 2, k * P:(k + 1) * P], IDF[:, :])
                        t.then_inc(g_pt, 1)
                        pe.wait_ge(g_ptc, pe.snap(q * (2 * TPS) + 2 * i + 2))
                        if i:
                            pe.wait_ge(g_out, G + i)
                        for k in range(TPS):
                            t = mm(AVP[:, 0:P], GPT[:, i % 2, k * P:(k + 1) * P], GV[:, k, :], start=(k == 0), stop=(k == TPS - 1))
                        t.then_inc(g_av, 1)
                    pe.wait_ge(g_out, G + TPS)

            for half in range(2):
                if half == 1:
                    pe.wait_ge(outer_done, 1)
                    pe.wait_ge(late_in, 16 * N_LATE)
                    global_attention()
                first_tile(half * (LAYERS * (TILES + 1) + 1) + 1)
                pe.wait_ge(mask_ready, 2)
                with pe.Fori(0, LAYERS) as l:
                    L = half * LAYERS + l
                    pe.wait_ge(wq_split, pe.snap(L * 3 + 3))
                    slot_loop(pe, L, half, slots)
                    ffn(L, half)

        @block.scalar
        def _(act):
            A = nc.scalar.activation
            act.wait_ge(const_ready, 6)

            def first_tile(count):
                act.wait_ge(xT_done, count)
                A(XTH[:, 0, :], VPS[:, 256:384], ACT.Copy).then_inc(xT_high, 1)

            def slots(L, half, U, p, first, last):
                S, T = act.snap(U * UNROLL), act.snap(U * 2)
                S2 = act.snap(S * 2)
                XB = act.snap(T + L + half)
                for j in range(UNROLL):
                    b = j % 2
                    g, par = j % GROUPS, j // GROUPS
                    if not last:
                        act.wait_ge(qk_done, S + j + 1)
                        if not (first and j < 2):
                            act.wait_ge(summed, S + (j - 1))
                        A(SQ[:, b, :], QKP[:, :], ACT.Square).then_inc(squared, 1)
                        act.wait_ge(qkv_done, S + j + 1)
                        if not (first and j < UNROLL):
                            act.wait_ge(av_done, S + (j - UNROLL + 1))
                            act.wait_ge(vtail_ready, S + (j - UNROLL + 1))
                        A(V[:, par, g * GW:(g + 1) * GW], VPS[:, 0:GW], ACT.Copy).then_inc(v_ready, 1)
                    if active(j, LAG_EXP, first, last):
                        s = j - LAG_EXP
                        act.wait_ge(bias_ready, S + (s + 1))
                        if not (first and s < 2):
                            act.wait_ge(probsT_done, S + (s - 1))
                        if not (first and s < 4):
                            act.wait_ge(prevT_ready, S + (s - 3))
                        for hh in range(2):
                            for pr in range(2):
                                i = 2 * hh + pr
                                e = A(PR[:, s % 4, i, :], SP2[hh][:, pr * SPAN:(pr + 1) * SPAN], ACT.Exp, bias=BIAS[:, s % 2, i:i + 1],
                                      scale=RN[:, s % UNROLL, 2 * pr + hh:2 * pr + hh + 1], accum_out=SUM[:, s % 2, i:i + 1])
                            e.then_inc(exp_done, 1)
                    if g == GROUPS - 2 and not last:
                        act.wait_ge(xT_done, XB + par + 2)
                    if active(j, LAG_AV, first, last):
                        s = j - LAG_AV
                        act.wait_ge(av_done, S + (s + 1))
                        if not (first and s < 2):
                            act.wait_ge(wo_done, S + s)
                        A(OT[:, s % 2, :, :], AVP[:, 0:2 * P].rearrange("p (a b) -> p a b", a=2), ACT.Copy).then_inc(outT_ready, 1)
                    if g == GROUPS - 2 and not last:
                        A(XTH[:, 1 - par, :], AVP[:, 256:384], ACT.Copy).then_inc(xT_high, 1)
                    if active(j, LAG_PT, first, last):
                        s = j - LAG_PT
                        act.wait_ge(probsT_done, S + (s + 1))
                        if not (first and s < 2):
                            act.wait_ge(av_done, S + (s - 1))
                        A(PT[:, s % 2, :, :], PTPS[:, :].rearrange("p (a b) -> p a b", a=GH), ACT.Copy).then_inc(probsT_ready, 1)
                    if active(j, LAG_T, first, last):
                        s = j - LAG_T
                        sg, spar = s % GROUPS, (s // GROUPS) % 2
                        act.wait_ge(rotT_done, S + (s + 1))
                        if not (first and s < 2):
                            act.wait_ge(scores_done, S2 + (2 * s - 2))
                        A(QT[:, s % 2, :, :], TPS_[:, 0:2 * P].rearrange("p (a b) -> p a b", a=2), ACT.Copy)
                        kps = TPS_[:, 2 * P:4 * P].rearrange("p (a b) -> p a b", a=2)
                        if spar:
                            A(KT[:, sg * 2:sg * 2 + 2, 0:WIN], kps[:, :, P - WIN:P], ACT.Copy, scale=KEEP[:, bass.ds(p + (s // UNROLL), 1)])
                        A(KT[:, sg * 2:sg * 2 + 2, WIN + spar * P:WIN + (spar + 1) * P], kps, ACT.Copy).then_inc(qkT_ready, 1)
                    if active(j, LAG_TAIL, first, last):
                        s = j - LAG_TAIL
                        sg, spar = s % GROUPS, (s // GROUPS) % 2
                        cols = slice(sg * GW, (sg + 1) * GW)
                        act.wait_ge(v_ready, S + (s + 1))
                        if not first:
                            act.wait_ge(av_done, S + (s - GROUPS + 2))
                        A(VP[0:WIN, 1 - spar, cols], V[P - WIN:P, spar, cols], ACT.Copy).then_inc(vtail_ready, 1)

            def ffn(L, half):
                C, C3 = act.snap(L * CHUNKS), act.snap(L * (3 * CHUNKS))
                act.wait_ge(lvec_ready, act.snap(L * 3 + 3))
                for c in range(CHUNKS):
                    act.wait_ge(xnT_done, C + (c + 1))
                    if c >= 2:
                        act.wait_ge(w1_done, C3 + 3 * (c - 1))
                    A(XNT[:, c % 2, :], XNP[:, :], ACT.Identity, scale=LVEC[:, 0:1], bias=LVEC[:, 1:2]).then_inc(xnT_ready, 1)
                    for k, (lo, n) in enumerate(HCH):
                        act.wait_ge(w1_done, C3 + (3 * c + k + 1))
                        if c:
                            act.wait_ge(hT_ready, C3 + (3 * (c - 1) + k + 1))
                        A(GL[0:n, k, :], GATE[k][0:n, :], ACT.Gelu, bias=BVEC[0:n, k, 1:2]).then_inc(gelu_ready, 1)
                first_tile(act.snap(L * (TILES + 1) + (TILES + 2 + half)))

            def global_attention():
                act.wait_ge(waT_done, 1)
                A(WAT[:, :, :], SA[:, 0:3 * P].rearrange("p (a b) -> p a b", a=3), ACT.Copy).then_inc(waT_ready, 1)
                with act.Fori(0, SEQS) as q:
                    G = act.snap(q * TPS)
                    act.wait_ge(g_xT, q + 1)
                    for n in range(2):
                        A(GXT[:, 4 * n:4 * n + 4, :], SP2[n][:, :].rearrange("p (a b) -> p a b", a=4), ACT.Copy).then_inc(g_xTc, 1)
                    act.wait_ge(g_proj, q + 1)
                    for n, bank in enumerate((QKP, VPS)):
                        A(GQT[:, n * 512:(n + 1) * 512], bank[:, :], ACT.Copy).then_inc(g_projc, 1)
                    A(GV[:, 0:4, :], AVP[:, :].rearrange("p (a b) -> p a b", a=4), ACT.Copy).then_inc(g_projc, 1)
                    for i in range(TPS):
                        act.wait_ge(g_max, G + (i + 1))
                        if i >= 2:
                            act.wait_ge(g_pt, G + (i - 1))
                            act.wait_ge(g_rs, G + (i - 1))
                        banks = [[SA, SB_], [QKP, VPS]][i % 2]
                        for n in range(2):
                            e = A(GP[:, i % 2, n * 512:(n + 1) * 512], banks[n][:, :], ACT.Exp, bias=GMX[:, i % 2:i % 2 + 1],
                                  accum_out=BIAS[:, i % 2, n:n + 1])
                        e.then_inc(g_exp, 1)
                        act.wait_ge(g_pt, G + (i + 1))
                        if i >= 2:
                            act.wait_ge(g_av, G + (i - 1))
                        A(GPT[:, i % 2, 0:512], TPS_[:, :], ACT.Copy).then_inc(g_ptc, 1)

            for half in range(2):
                if half == 1:
                    global_attention()
                first_tile(half * (LAYERS * (TILES + 1) + 1) + 1)
                with act.Fori(0, LAYERS) as l:
                    L = half * LAYERS + l
                    slot_loop(act, L, half, slots)
                    ffn(L, half)

        @block.vector
        def _(dve):
            dve.wait_ge(x_in, 16)
            dve.wait_ge(const_ready, 6)

            links = [0, 0]

            def link(ins):
                ins.then_inc(ln_link, 1)
                links[1] += 1

            def linked():
                dve.wait_ge(ln_link, links[0] + links[1])

            def statistics_steps(src, lo, hi):
                for t in range(lo, hi):
                    stats = dve.bn_stats(ST[:, t, :], src[:, t, :])
                    if t % 2:
                        yield
                link(stats)
                linked()
                lt, lv, r = LT[:, lo:hi], LV[:, lo:hi], RSTD[:, lo:hi]
                dve.memset(lt, 0.0)
                for t in range(lo, hi):
                    agg = dve.bn_aggr(MV[:, t, :], ST[:, t, :])
                    if t % 4 == 3:
                        yield
                link(agg)
                yield
                linked()
                link(dve.tensor_scalar(lv, MV[:, lo:hi, 1], 1e-5, None, ALU.add))
                yield
                linked()
                link(dve.tensor_scalar(r.bitcast(I32), lv.bitcast(I32), -0.5, MAGIC, ALU.mult, ALU.add))
                for _ in range(NEWTON):
                    yield
                    linked()
                    link(dve.scalar_tensor_tensor(lt, r, -0.5, r, ALU.mult, ALU.mult))
                    yield
                    linked()
                    link(dve.tensor_tensor(lt, lt, lv, ALU.mult))
                    yield
                    linked()
                    link(dve.scalar_tensor_tensor(r, lt, 1.5, r, ALU.add, ALU.mult))
                yield
                linked()

            def statistics(src, lo=0, hi=TILES):
                for _ in statistics_steps(src, lo, hi):
                    pass

            STAT_LINKS = 4 + 3 * NEWTON
            EARLY = TILES - CT

            def normalize(dst, src, t):
                return dve.tensor_scalar(dst, src, MV[:, t, 0:1], RSTD[:, t:t + 1], ALU.subtract, ALU.mult)

            def enter_stack(half):
                statistics(XO)
                for c in range(CHUNKS):
                    if c == 2:
                        dve.wait_ge(shift_a[0], half * (LAYERS + 1) * 16 * CHUNKS + 32)
                        stage_first()
                    for t in range(c * CT, (c + 1) * CT):
                        dve.tensor_scalar(XSA[:, t, 0:DH], XO[:, t, 0:DH], MV[:, t, 0:1], RSTD[:, t:t + 1], ALU.subtract, ALU.mult)
                        w = normalize(X[:, t, :], XO[:, t, :], t)
                    w.then_inc(x_chunk, 1)
                    if c == 2:
                        first_low(half * (LAYERS * (TILES + 1) + 1) + 1)

            def norm_chunk(C, c):
                if c >= 2:
                    dve.wait_ge(xnT_done, C + (c - 1))
                for t in range(c * CT, (c + 1) * CT):
                    n = normalize(XN[:, c % 2, t - c * CT, :], XSF[:, t, :], t)
                n.then_inc(xn_ready, 1)

            def ffn_start(L, l, half):
                dve.wait_ge(late_in, 16 * N_LATE)
                dve.tensor_copy(LVEC[:, 0:1], LNG[:, bass.ds(l, 1)]).then_inc(lvec_ready, 1)
                dve.tensor_copy(LVEC[:, 1:2], LNB[:, bass.ds(l, 1)]).then_inc(lvec_ready, 1)
                dve.tensor_copy(BVEC[:, :, :], B1[:, :, bass.ds(l, 1), :].rearrange("p k a c -> p k (a c)")).then_inc(lvec_ready, 1)
                dve.tensor_copy(B2L[:, :].rearrange("p (a b) -> p a b", a=1), B2[:, bass.ds(l, 1), :])
                yield
                for i in range(2):
                    dve.wait_ge(shift_f[i], dve.snap(L * (32 * ITERS) + 32 * (ITERS - 1)))
                links[0], links[1] = dve.snap(L * (2 * STAT_LINKS) + (1 + 2 * half) * STAT_LINKS), 0
                for _ in statistics_steps(XSF, 0, EARLY):
                    yield
                C = dve.snap(L * CHUNKS)
                norm_chunk(C, 0)
                yield
                norm_chunk(C, 1)

            def slots(L, half, U, p, first, last, early=None):
                S, T = dve.snap(U * UNROLL), dve.snap(U * 2)
                R, S2 = dve.snap(S * RN_STEPS), dve.snap(S * 2)
                if not last:
                    tq = 0 if first else dve.snap((p % (TPS // 2)) * 2)

                def rn_steps(s):
                    b, rn = s % 2, RN[:, s % UNROLL, :]
                    k = s * RN_STEPS

                    def after(n):
                        dve.wait_ge(rn_step, R + (k + n))
                    dve.wait_ge(summed, S + (s + 1))
                    dve.tensor_scalar(SSC[:, b, :], SS[:, b, :], 1e-24, None, ALU.max).then_inc(rn_step, 1)
                    yield
                    after(1)
                    if not (first and s < UNROLL):
                        dve.wait_ge(exp_done, S2 + (2 * (s - UNROLL) + 4))
                    dve.tensor_scalar(rn.bitcast(I32), SSC[:, b, :].bitcast(I32), -0.5, MAGIC, ALU.mult, ALU.add).then_inc(rn_step, 1)
                    for it in range(NEWTON):
                        yield
                        after(2 + 3 * it)
                        dve.scalar_tensor_tensor(NT[:, :], rn, -0.5, rn, ALU.mult, ALU.mult).then_inc(rn_step, 1)
                        yield
                        after(3 + 3 * it)
                        dve.tensor_tensor(NT[:, :], NT[:, :], SSC[:, b, :], ALU.mult).then_inc(rn_step, 1)
                        yield
                        after(4 + 3 * it)
                        dve.scalar_tensor_tensor(rn, NT[:, :], 1.5, rn, ALU.add, ALU.mult).then_inc(rn_step, 1)

                def slot(j, step, burst):
                    b = j % 2
                    g, par = j % GROUPS, j // GROUPS
                    step()
                    if not last:
                        dve.wait_ge(squared, S + j + 1)
                        if not (first and j < 2):
                            dve.wait_ge(rot_added, S + (j - 1))
                        raw = QKP[:, :].rearrange("p (a h d) -> p a h d", a=2, h=GH)
                        qc = QKC[:, b, :].rearrange("p (a h d) -> p a h d", a=2, h=GH)
                        qs = QKS[:, b, :].rearrange("p (a h d) -> p a h d", a=2, h=GH)
                        HF = DH // 2

                        def tab(t, lo, n):
                            v = t[:, bass.ds(tq + par, 1), :].rearrange("p o (a d) -> p (o a) d", a=2)[:, :, lo:lo + n]
                            return v.unsqueeze(2).to_broadcast([P, 2, GH, n])
                        dve.tensor_tensor(qc, raw, tab(TABC, 0, DH), ALU.mult)
                        step()
                        dve.tensor_tensor(qs[:, :, :, 0:HF], raw[:, :, :, HF:DH], tab(TABS, 0, HF), ALU.mult)
                        step()
                        dve.tensor_tensor(qs[:, :, :, HF:DH], raw[:, :, :, 0:HF], tab(TABS, HF, HF), ALU.mult).then_inc(rotprod_done, 1)
                        step()
                    if g == 1 and not last:
                        if first and par == 0:
                            for c in range(2):
                                dve.wait_ge(shift_a[c], dve.snap((L + half + 1) * (16 * CHUNKS)))
                        if not (first and par == 0):
                            dve.wait_ge(xT_done, dve.snap(T + L + half) + par)
                        dve.tensor_scalar(XST[:, 1 - par:2 - par, :], XSA[:, bass.ds(p * 2 + par + 1, 1), :], 1.0, None, ALU.mult).then_inc(xs_staged, 1)
                    if active(j, LAG_EXP, first, last):
                        s = j - LAG_EXP
                        dve.wait_ge(exp_done, S2 + (2 * s + 2))
                        if not (first and s < 2):
                            dve.wait_ge(probs_ready, S + (s - 1))
                        dve.reciprocal(RSUM[:, s % 2, :], SUM[:, s % 2, :]).then_inc(recip_done, 1)
                    step()
                    if active(j, LAG_PT, first, last):
                        s = j - LAG_PT
                        dve.wait_ge(probs_ready, S + (s + 1))
                        if not (first and s < 2):
                            dve.wait_ge(av_done, S + (s - 1))
                        dve.transpose(PTP[0:WIN, s % 2, :, :], PR[0:WIN, s % 4, :, 0:WIN]).then_inc(prevT_ready, 1)
                    step()
                    if active(j, LAG_S, first, last):
                        s = j - LAG_S
                        for hh in range(2):
                            dve.wait_ge(scores_done, S2 + (2 * s + 1 + hh))
                            dve.tensor_reduce(MX[:, s % 2, 2 * hh:2 * hh + 2], SP2[hh][:, 0:2 * SPAN].rearrange("p (h c) -> p h c", h=2), AX.X, ALU.max).then_inc(max_done, 1)
                            step()
                        dve.wait_ge(max_done, S2 + (2 * s + 2))
                        dve.scalar_tensor_tensor(BIAS[:, s % 2, :].rearrange("p (a b) -> p a b", a=2), MX[:, s % 2, :].rearrange("p (a b) -> p a b", a=2), -1.0,
                                                 RN[:, s % UNROLL, 0:GH].rearrange("p (b a) -> p a b", a=2), ALU.mult, ALU.mult).then_inc(bias_ready, 1)
                    burst()
                    if g == GROUPS - 2 and not last:
                        dve.wait_ge(xT_high, dve.snap(T + L + half) + (par + 2))
                        dve.tensor_tensor(XTL[:, 1 - par, :], AVP[:, 256:384], XTH[:, 1 - par, :], ALU.subtract).then_inc(xT_low, 1)
                    step()
                    if not last:
                        dve.tensor_reduce(SS[:, b, :], SQ[:, b, :].rearrange("p (h d) -> p h d", d=DH), AX.X, ALU.add).then_inc(summed, 1)
                    step()
                    if active(j, LAG_WO, first, last) and (j - LAG_WO) % GROUPS == GROUPS - 1:
                        s = j - LAG_WO
                        tt = p * 2 + (s // GROUPS)
                        dve.wait_ge(wo_done, S + (s + 2))
                        o = WOP[:, 0:P].rearrange("p (a b) -> p a b", a=1)
                        xt = X[:, bass.ds(tt, 1), :]
                        odd = (s // GROUPS) % 2
                        dve.tensor_tensor(XSF[:, bass.ds(tt, 1), 0:DH], o[:, :, 0:DH], xt[:, :, 0:DH], ALU.add).then_inc(half_f, 1)
                        if odd:
                            cp = p + (s // UNROLL)
                            rows = slice(P - WIN, P)
                            dve.tensor_tensor(CARRY[rows, bass.ds(cp, 1), :], o[rows, :, DH:P], X[rows, bass.ds(tt, 1), DH:P], ALU.add).then_inc(carried, 1)
                            dve.wait_ge(carried, dve.snap(U * 2 + ((s // UNROLL) * 2 + 1)))
                            dve.tensor_scalar(CARRY[rows, bass.ds(cp, 1), :], CARRY[rows, bass.ds(cp, 1), :], KEEP[rows, bass.ds(cp, 1)], None, ALU.mult).then_inc(carried, 1)
                        step()
                        dve.wait_ge(half_f, T + (s // GROUPS + 1))
                        dve.tensor_tensor(xt, o, xt, ALU.add).then_inc(x_tile, 1)
                    for _ in range(RN_STEPS):
                        step()

                for j in range(UNROLL):
                    steps = rn_steps(j - 1) if active(j, 1, first, last) else iter(())
                    count = 0 if not last else 5 if j < LAG_S else RN_STEPS
                    slot(j, lambda: next(steps, None), lambda: [next(early, None) for _ in range(count)])

            def ffn(L, l, half):
                C, C3 = dve.snap(L * CHUNKS), dve.snap(L * (3 * CHUNKS))
                def update(c):
                    dve.wait_ge(y_done, C + (c + 1))
                    dve.tensor_tensor(YB[:, c % 2, :, :], YP[:, :].rearrange("p (a b) -> p a b", a=CT), B2L[:, :].unsqueeze(1).to_broadcast([P, CT, P]), ALU.add).then_inc(yb_ready, 1)
                    dve.wait_ge(yb_ready, C + (c + 1))
                    tt = slice(c * CT, (c + 1) * CT)
                    dve.tensor_tensor(XSA[:, tt, 0:DH], YB[:, c % 2, :, 0:DH], X[:, tt, 0:DH], ALU.add).then_inc(half_a, 1)
                    dve.wait_ge(half_a, C + (c + 1))
                    dve.tensor_tensor(X[:, tt, :], YB[:, c % 2, :, :], X[:, tt, :], ALU.add).then_inc(x_chunk, 1)

                for c in range(CHUNKS):
                    if c >= 2:
                        dve.wait_ge(y_done, C + (c - 1))
                    for k, (lo, n) in enumerate(HCH):
                        dve.wait_ge(gelu_ready, C3 + (3 * c + k + 1))
                        dve.scalar_tensor_tensor(HT[0:n, c % 2, k, :], LIN[k][0:n, :], BVEC[0:n, k, 0:1], GL[0:n, k, :], ALU.add, ALU.mult).then_inc(hT_ready, 1)
                    if c == 0:
                        norm_chunk(C, 2)
                        for i in range(2):
                            dve.wait_ge(shift_f[i], dve.snap(L * (32 * ITERS) + 32 * ITERS))
                        statistics(XSF, EARLY, TILES)
                        norm_chunk(C, 3)
                    if c == CHUNKS - 1:
                        dve.wait_ge(shift_a[0], dve.snap((half * (LAYERS + 1) + 1 + l) * (16 * CHUNKS) + 32))
                        stage_first()
                    if c:
                        update(c - 1)
                first_low(dve.snap(L * (TILES + 1) + (TILES + 2 + half)))
                update(CHUNKS - 1)

            def stage_first():
                dve.tensor_scalar(XST[:, 0, :], XSA[:, 0, :], 1.0, None, ALU.mult).then_inc(xs_staged, 1)

            def first_low(count):
                dve.wait_ge(xT_high, count)
                dve.tensor_tensor(XTL[:, 0, :], VPS[:, 256:384], XTH[:, 0, :], ALU.subtract).then_inc(xT_low, 1)

            def leave_stack(n):
                dve.wait_ge(x_chunk, n)
                dve.scalar_tensor_tensor(XO[:, :, :], X[:, :, :], 0.5, XO[:, :, :], ALU.mult, ALU.add).then_inc(outer_done, 1)

            def global_attention():
                with dve.Fori(0, SEQS) as q:
                    G = dve.snap(q * TPS)
                    for i in range(TPS):
                        t = q * TPS + i
                        n = dve.tensor_scalar(GX[:, i:i + 1, :], XO[:, bass.ds(t, 1), :], MV[:, bass.ds(t, 1), 0:1].rearrange("p a b -> p (a b)"),
                                              RSTD[:, bass.ds(t, 1)], ALU.subtract, ALU.mult)
                    n.then_inc(g_xn, 1)
                    dve.wait_ge(g_proj, q + 1)
                    for n, bank in enumerate((TPS_, PTPS)):
                        dve.tensor_copy(GKT[:, n * 512:(n + 1) * 512], bank[:, :]).then_inc(g_projc, 1)
                    dve.tensor_copy(GV[:, 4:8, :], WOP[:, :].rearrange("p (a b) -> p a b", a=4)).then_inc(g_projc, 1)

                    def finish(i):
                        dve.wait_ge(g_av, G + (i + 1))
                        dve.wait_ge(g_rs, G + (i + 1))
                        xt = XO[:, bass.ds(q * TPS + i, 1), :]
                        dve.scalar_tensor_tensor(xt, AVP[:, 0:P].rearrange("p (a b) -> p a b", a=1), GRS[:, i % 2:i % 2 + 1], xt, ALU.mult, ALU.add).then_inc(g_out, 1)

                    made = [0]

                    def linked_to(ins):
                        ins.then_inc(g_link, 1)
                        made[0] += 1
                        dve.wait_ge(g_link, dve.snap(q * (4 * TPS) + made[0]))

                    def row_max(i):
                        dve.wait_ge(g_s, G + (i + 1))
                        banks = [[SA, SB_], [QKP, VPS]][i % 2]
                        for n in range(2):
                            m = dve.tensor_reduce(MX[:, i % 2, n:n + 1], banks[n][:, :], AX.X, ALU.max)
                        linked_to(m)
                        if i >= 2:
                            dve.wait_ge(g_exp, G + (i - 1))
                        gm = GMX[:, i % 2:i % 2 + 1]
                        linked_to(dve.tensor_tensor(gm, MX[:, i % 2, 0:1], MX[:, i % 2, 1:2], ALU.max))
                        dve.tensor_scalar(gm, gm, -1.0, None, ALU.mult).then_inc(g_max, 1)

                    row_max(0)
                    for i in range(TPS):
                        dve.wait_ge(g_exp, G + (i + 1))
                        linked_to(dve.tensor_tensor(GSUM[:, i % 2:i % 2 + 1], BIAS[:, i % 2, 0:1], BIAS[:, i % 2, 1:2], ALU.add))
                        linked_to(dve.reciprocal(GRS[:, i % 2:i % 2 + 1], GSUM[:, i % 2:i % 2 + 1]))
                        dve.tensor_scalar(GRS[:, i % 2:i % 2 + 1], GRS[:, i % 2:i % 2 + 1], NORM, None, ALU.mult).then_inc(g_rs, 1)
                        dve.wait_ge(g_pt, G + (i + 1))
                        if i >= 2:
                            dve.wait_ge(g_av, G + (i - 1))
                        dve.tensor_copy(GPT[:, i % 2, 512:1024], PTPS[:, :]).then_inc(g_ptc, 1)
                        if i + 1 < TPS:
                            row_max(i + 1)
                        finish(i)

            enter_stack(0)
            dve.wait_ge(const_in, 16 * N_CONST)
            dve.tensor_copy(IDB[:, :], IDF[:, :]).then_inc(x_tile, 1)
            dve.tensor_copy(MASKO[:, 0, :], MRAW[:, 1, :]).then_inc(wo_done, 1)
            for i in range(2):
                if i:
                    dve.tensor_copy(MASKO[:, i, :], MRAW[:, 1, :])
                for a in range(0, ITERS, TPS // 2):
                    dve.tensor_copy(MASK[:, a + 1:a + TPS // 2, i, :], MRAW[:, 1:2, :].to_broadcast([P, TPS // 2 - 1, SPAN]))
            for i in range(2):
                dve.tensor_copy(MASK[:, 0:ITERS:TPS // 2, i, :], MRAW[:, 0:1, :].to_broadcast([P, 2, SPAN])).then_inc(mask_ready, 1)
            for half in range(2):
                if half == 1:
                    links[0], links[1] = 0, (2 * LAYERS + 1) * STAT_LINKS
                    dve.wait_ge(outer_done, 1)
                    statistics(XO)
                    global_attention()
                    dve.wait_ge(g_out, TILES)
                    dve.tensor_copy(LT[:, 0:1], ROPEC[:, 0, 0:1]).then_inc(outer_done, 1)
                    for c in range(2):
                        dve.wait_ge(shift_a[c], (LAYERS + 1) * 16 * CHUNKS)
                    enter_stack(half)
                with dve.Fori(0, LAYERS) as l:
                    L = half * LAYERS + l
                    dve.wait_ge(tab_ready, dve.snap(L * 2 + 2))
                    early = ffn_start(L, l, half)
                    slot_loop(dve, L, half, lambda *a: slots(*a, early=early))
                    for _ in early:
                        pass
                    ffn(L, l, half)
                leave_stack((half + 1) * (LAYERS + 1) * CHUNKS)


def rotary_constants():
    f = np.float32
    half = np.arange(0, DH, 2, dtype=f)
    inv_freq = (f(1.0) / f(10000.0) ** (half / f(DH))).astype(f)
    t = np.arange(SEQ, dtype=f)
    freqs = t[:, None] * inv_freq[None, :]
    base = (half + f(0.4 * DH)) / f(1.4 * DH)
    scale = base[None, :] ** ((t - f(SEQ // 2)) / f(WIN // 2))[:, None]
    cos, sin = np.cos(freqs), np.sin(freqs)
    sign_sin = np.concatenate([-sin, sin], -1)
    cos, scale = np.concatenate([cos, cos], -1), np.concatenate([scale, scale], -1)
    c = np.concatenate([8 * cos * scale, cos * (1 / scale)], -1)
    s = np.concatenate([8 * sign_sin * scale, sign_sin * (1 / scale)], -1)
    return [np.ascontiguousarray(a.astype(f).reshape(TPS, P, P).transpose(1, 0, 2)) for a in (c, s)]


def mask_constants():
    i, key = np.arange(P)[:, None], np.arange(SPAN)[None, :] - WIN
    seen = (i >= key) & (i - key <= WIN)
    both = np.stack([seen & (key >= 0), seen], 1)
    return np.where(both, 0.0, NEG).astype(np.float32)


def kernel(**inputs):
    import concourse.bacc as bacc
    from concourse.bass_utils import run_bass_kernel_spmd

    i = {k: np.asarray(v) for k, v in inputs.items()}
    swap = np.concatenate([np.arange(DH // 2, DH), np.arange(DH // 2)])
    cos, sin = rotary_constants()
    qs, ks = i["L0_ffn_q_scale"], i["L0_ffn_k_scale"]
    arrays = {
        "x": i["L0_attn_x"], "wq": i["L0_attn_Wq"], "wk": i["L0_attn_Wk"], "wv": i["L0_attn_Wv"],
        "wqkv": i["L0_ffn_Wqkv"],
        "qk_rows": np.concatenate([qs, ks], 1), "qk_swap_rows": np.concatenate([qs[:, swap], ks[:, swap]], 1),
        "wo": i["L0_ffn_Wo"], "ln_g": i["L0_ffn_ln_g"].T, "ln_b": i["L0_ffn_ln_b"].T, "w1": i["L0_ffn_W1"],
        "b1": i["L0_ffn_b1"].reshape(LAYERS, 2, HID).transpose(2, 0, 1), "w2": i["L0_ffn_W2"], "b2": i["L0_ffn_b2"],
        "rope_cos": cos, "rope_sin": sin, "ident": np.eye(P, dtype=np.float32), "masks": mask_constants(),
    }
    arrays = {k: np.ascontiguousarray(v) for k, v in arrays.items()}
    nc = bacc.Bacc("TRN2", target_bir_lowering=False, num_devices=1)
    args = [nc.dram_tensor(k, v.shape, F32, kind="ExternalInput").ap() for k, v in arrays.items()]
    out = nc.dram_tensor("y", (SEQS, SEQ, P), F32, kind="ExternalOutput").ap()
    build(nc, *args, out)
    r = run_bass_kernel_spmd(nc, [arrays], core_ids=[0])
    return r.results[0]["y"]
```
